# Optimizing a Trainium2 kernel written in Bass

```python
import numpy as np
import jax
import jax.numpy as jnp

def _softmax(x, axis=-1):
    return jax.nn.softmax(x, axis=axis)

def _gelu(x):
    return jax.nn.gelu(x, approximate=True)

def _silu(x):
    return jax.nn.silu(x)

def _sigmoid(x):
    return jax.nn.sigmoid(x)

def _layernorm(x, axis=-1, eps=1e-05):
    m = jnp.mean(x, axis=axis, keepdims=True)
    v = jnp.var(x, axis=axis, keepdims=True)
    return (x - m) / jnp.sqrt(v + eps)

def _scatter_add(tgt, idx, src, axis=0):
    return tgt.at[idx].add(src)

def _segment_sum(src, seg, n):
    return jax.ops.segment_sum(src, seg, n)
kernel_name = 'mk_prb_d1_jaxref_r4_59cea6'

def setup_inputs(seed: int=0):
    np.random.seed(seed)
    _w = jnp.asarray

    def _L0_attn_setup():
        import jax, jax.numpy as jnp
        import numpy as np
        D_MODEL = 512
        NUM_HEADS = 16
        HEAD_DIM = D_MODEL // NUM_HEADS
        LAYER_IDX = 0
        NUM_LAYERS = 13
        REINIT_LAMBDA = 0.8

        def _heads(t, B, S):
            return t.reshape(B, S, NUM_HEADS, HEAD_DIM).transpose(0, 2, 1, 3)
        key = jax.random.key(seed)
        ks = jax.random.split(key, 8)
        B, S = (2, 512)
        x = jax.random.normal(ks[0], (B, S, D_MODEL), dtype=jnp.float32)
        init = 1.0 / np.sqrt(D_MODEL)

        def w(k):
            return jax.random.uniform(k, (D_MODEL, D_MODEL), dtype=jnp.float32, minval=-init, maxval=init)
        lam_init = REINIT_LAMBDA * ((LAYER_IDX + 1) / NUM_LAYERS)
        return {'x': x, 'q1_w': w(ks[1]), 'k1_w': w(ks[2]), 'q2_w': w(ks[3]), 'k2_w': w(ks[4]), 'v_w': w(ks[5]), 'o_w': w(ks[6]), 'lambda_param': jnp.full((NUM_HEADS,), lam_init, dtype=jnp.float32)}
    _L0_attn_in = _L0_attn_setup()

    def _L0_ffn_setup():
        import jax, jax.numpy as jnp
        import numpy as np
        B, S, H = (1, 256, 512)
        E, K = (32, 4)
        F, FS = (352, 1408)
        CAP = 64

        def silu(x):
            return x * jax.nn.sigmoid(x)
        key = jax.random.key(seed)
        ks = jax.random.split(key, 9)
        sc = 0.02
        return {'hidden_states': jax.random.normal(ks[0], (B, S, H), jnp.float32), 'Wr': jax.random.normal(ks[1], (H, E), jnp.float32) * sc, 'Wg': jax.random.normal(ks[2], (E, H, F), jnp.float32) * sc, 'Wu': jax.random.normal(ks[3], (E, H, F), jnp.float32) * sc, 'Wd': jax.random.normal(ks[4], (E, F, H), jnp.float32) * sc, 'Wsg': jax.random.normal(ks[5], (H, FS), jnp.float32) * sc, 'Wsu': jax.random.normal(ks[6], (H, FS), jnp.float32) * sc, 'Wsd': jax.random.normal(ks[7], (FS, H), jnp.float32) * sc, 'Wse': jax.random.normal(ks[8], (H, 1), jnp.float32) * sc}
    _L0_ffn_in = _L0_ffn_setup()
    _d = {'L0_attn_x': _L0_attn_in['x'], 'L0_attn_q1_w': _L0_attn_in['q1_w'], 'L0_attn_k1_w': _L0_attn_in['k1_w'], 'L0_attn_q2_w': _L0_attn_in['q2_w'], 'L0_attn_k2_w': _L0_attn_in['k2_w'], 'L0_attn_v_w': _L0_attn_in['v_w'], 'L0_attn_o_w': _L0_attn_in['o_w'], 'L0_attn_lambda_param': _L0_attn_in['lambda_param'], 'L0_ffn_Wr': _L0_ffn_in['Wr'], 'L0_ffn_Wg': _L0_ffn_in['Wg'], 'L0_ffn_Wu': _L0_ffn_in['Wu'], 'L0_ffn_Wd': _L0_ffn_in['Wd'], 'L0_ffn_Wsg': _L0_ffn_in['Wsg'], 'L0_ffn_Wsu': _L0_ffn_in['Wsu'], 'L0_ffn_Wsd': _L0_ffn_in['Wsd'], 'L0_ffn_Wse': _L0_ffn_in['Wse']}
    _x0 = _d['L0_attn_x']
    _d['L0_attn_x'] = jax.random.normal(jax.random.fold_in(jax.random.key(seed), 1), (2, 2048, 512), dtype=_x0.dtype)
    del _x0
    return _d

def reference(L0_attn_x, L0_attn_q1_w, L0_attn_k1_w, L0_attn_q2_w, L0_attn_k2_w, L0_attn_v_w, L0_attn_o_w, L0_attn_lambda_param, L0_ffn_Wr, L0_ffn_Wg, L0_ffn_Wu, L0_ffn_Wd, L0_ffn_Wsg, L0_ffn_Wsu, L0_ffn_Wsd, L0_ffn_Wse):

    def _L0_attn_ref(x, q1_w, k1_w, q2_w, k2_w, v_w, o_w, lambda_param):
        import jax, jax.numpy as jnp
        import numpy as np
        D_MODEL = 512
        NUM_HEADS = 16
        HEAD_DIM = D_MODEL // NUM_HEADS
        LAYER_IDX = 0
        NUM_LAYERS = 13
        REINIT_LAMBDA = 0.8

        def _heads(t, B, S):
            return t.reshape(B, S, NUM_HEADS, HEAD_DIM).transpose(0, 2, 1, 3)
        B, S, _ = x.shape
        q1 = _heads(x @ q1_w.T, B, S)
        k1 = _heads(x @ k1_w.T, B, S)
        q2 = _heads(x @ q2_w.T, B, S)
        k2 = _heads(x @ k2_w.T, B, S)
        v = _heads(x @ v_w.T, B, S)
        scale = jnp.sqrt(jnp.float32(HEAD_DIM))
        attn1 = jax.nn.softmax(jnp.einsum('bhqd,bhkd->bhqk', q1, k1) / scale, axis=-1)
        attn2 = jax.nn.softmax(jnp.einsum('bhqd,bhkd->bhqk', q2, k2) / scale, axis=-1)
        lam = lambda_param.reshape(1, NUM_HEADS, 1, 1)
        out = jnp.einsum('bhqk,bhkd->bhqd', attn1 - lam * attn2, v)
        out = out.transpose(0, 2, 1, 3).reshape(B, S, D_MODEL)
        return out @ o_w.T

    def _L0_ffn_ref(hidden_states, Wr, Wg, Wu, Wd, Wsg, Wsu, Wsd, Wse):
        import jax, jax.numpy as jnp
        import numpy as np
        B, S, H = (1, 256, 512)
        E, K = (32, 4)
        F, FS = (352, 1408)
        CAP = 64

        def silu(x):
            return x * jax.nn.sigmoid(x)
        b, s_len, h = hidden_states.shape
        x = hidden_states.reshape(-1, h)
        T = x.shape[0]
        probs = jax.nn.softmax(x @ Wr, axis=-1)
        topw, topi = jax.lax.top_k(probs, K)
        topw = topw / jnp.sum(topw, axis=-1, keepdims=True)
        shared = silu(x @ Wsg) * (x @ Wsu) @ Wsd
        shared = shared * jax.nn.sigmoid(x @ Wse)
        sel = topi.reshape(-1)
        w = topw.reshape(-1)
        tok = jnp.repeat(jnp.arange(T), K)
        oh = jax.nn.one_hot(sel, E, dtype=jnp.int32)
        pos = (jnp.cumsum(oh, axis=0) * oh).sum(-1) - 1
        valid = (pos < CAP).astype(x.dtype)
        posc = jnp.clip(pos, 0, CAP - 1)
        xe = jnp.zeros((E, CAP, h), x.dtype).at[sel, posc].add(x[tok] * valid[:, None])
        g = silu(jnp.einsum('ech,ehf->ecf', xe, Wg))
        u = jnp.einsum('ech,ehf->ecf', xe, Wu)
        ye = jnp.einsum('ecf,efh->ech', g * u, Wd)
        y_pair = ye[sel, posc] * (w * valid)[:, None]
        out = shared.at[tok].add(y_pair)
        return out.reshape(b, s_len, h)
    x = L0_attn_x
    xn = _layernorm(x, axis=-1)
    x = x + _L0_attn_ref(xn, L0_attn_q1_w, L0_attn_k1_w, L0_attn_q2_w, L0_attn_k2_w, L0_attn_v_w, L0_attn_o_w, L0_attn_lambda_param) + _L0_ffn_ref(xn, L0_ffn_Wr, L0_ffn_Wg, L0_ffn_Wu, L0_ffn_Wd, L0_ffn_Wsg, L0_ffn_Wsu, L0_ffn_Wsd, L0_ffn_Wse)
    return x

_drawn_inputs = setup_inputs


def setup_inputs(seed=0):
    import zlib

    import numpy as np

    out = dict(_drawn_inputs(seed))
    spreads = {'L0_attn_lambda_param': (0.0615384615957737, 0.6)}
    factors = {'L0_attn_q1_w': 8.0,
     'L0_attn_k1_w': 8.0,
     'L0_attn_q2_w': 8.0,
     'L0_attn_k2_w': 8.0,
     'L0_attn_v_w': 6.492,
     'L0_attn_o_w': 6.309,
     'L0_ffn_Wr': 8.0,
     'L0_ffn_Wg': 7.86,
     'L0_ffn_Wu': 7.695,
     'L0_ffn_Wd': 7.691,
     'L0_ffn_Wse': 53.712,
     'L0_ffn_Wsg': 8.0,
     'L0_ffn_Wsu': 8.0,
     'L0_ffn_Wsd': 8.0}
    for name, (base, spread) in spreads.items():
        noise = np.random.default_rng([zlib.crc32(name.encode()), seed]).standard_normal(out[name].shape)
        drawn = base * np.exp(spread * noise) if base else spread * noise
        out[name] = jnp.asarray(drawn.astype(out[name].dtype))
    for name, factor in factors.items():
        out[name] = (out[name] * factor).astype(out[name].dtype)
    return out
```

```python
from contextlib import ExitStack

import concourse.bass as bass
from concourse import mybir

ALU = mybir.AluOpType
ACT = mybir.ActivationFunctionType
F32 = mybir.dt.float32
F32R = mybir.dt.float32r
BF16 = mybir.dt.bfloat16
I32 = mybir.dt.int32
U32 = mybir.dt.uint32
AX_X = mybir.AxisListType.X

P = 128
B, S, D = 2, 2048, 512
H, DH = 16, 32
T = B * S
KT = D // P
BLK = 512
NBLK = T // BLK
BPB = S // BLK
TPB = BLK // P
HEADS = B * H
ITERS = HEADS * BPB
E, TOPK, CAP = 32, 4, 64
F, FS = 352, 1408
FT = 88
FN = F // FT
FSN = FS // P
ROW = D + 16
C_TOK, C_W, C_E = D, D + 1, D + 1 + TOPK
LN_EPS = 1e-5
FAR = 1.0e6
Q_SCALE = float(DH) ** -0.5
NG = 4 * KT
NGV = NG + TPB


def allocators(nc, ctx, stage):
    def sb(name, shape, dt=F32):
        return ctx.enter_context(nc.sbuf_tensor(f"{stage}_{name}", shape, dt))

    def ps(name, shape, dt=F32):
        return ctx.enter_context(nc.psum_tensor(f"{stage}_{name}", shape, dt))

    def sem(name):
        return ctx.enter_context(nc.semaphore(f"{stage}_{name}"))

    return sb, ps, sem


def stand(eng, passed):
    eng.sem_inc(passed, 1)


def linker(eng, order, per_round):
    done = [0]

    def link(ins, i):
        done[0] = done[0] % per_round + 1
        ins.then_inc(order, 1)
        eng.wait_ge(order, i * per_round + done[0])

    return link


def project(nc, x, w_dram, wr_dram, xe, xnt_d, qd, kd, vd, gate_d):
    with ExitStack() as ctx:
        sb, ps, sem = allocators(nc, ctx, "project")
        passed = sem("passed")
        NW = 5
        w = sb("w", [P, NW, KT, D])
        wr = sb("wr", [P, KT, E + 1])
        xin = sb("xin", [P, TPB, D])
        xn = sb("xn", [P, TPB, ROW])
        xnT = sb("xnT", [P, KT, BLK])
        ident = sb("ident", [P, P])
        before = sb("before", [P, P], BF16)
        ones = sb("ones", [P, P], BF16)
        e_iota = sb("e_iota", [P, E])
        e_slot = sb("e_slot", [P, E])
        iota_i = sb("iota_i", [P, E], I32)
        tok_i = sb("tok_i", [P, TPB], I32)
        tok_f = sb("tok_f", [P, TPB])
        blank = sb("blank", [P, ROW])
        dummy_i = sb("dummy_i", [P, 1], I32)
        stats = sb("stats", [P, TPB, 6])
        mv = sb("mv", [P, TPB, 2])
        std = sb("std", [P, TPB])
        rstd = sb("rstd", [P, TPB])
        eps = sb("eps", [P, 1])
        lg = sb("lg", [P, TPB, E + 1])
        top = sb("top", [P, TPB, 8])
        topi = sb("topi", [P, TPB, 8], U32)
        ntop = sb("ntop", [P, TPB])
        ex = sb("ex", [P, TPB, TOPK])
        exs = sb("exs", [P, TPB])
        exr = sb("exr", [P, TPB])
        se_e = sb("se_e", [P, TPB])
        gate = sb("gate", [P, NBLK * TPB])
        eq = sb("eq", [P, TPB, TOPK, E])
        mask = sb("mask", [P, TPB, E], BF16)
        carry = sb("carry", [P, E])
        carry_b = sb("carry_b", [P, E], BF16)
        blk_n = sb("blk_n", [P, E])
        over = sb("over", [P, TPB, E])
        slot = sb("slot", [P, TPB, E])
        picked = sb("picked", [P, TPB, TOPK, E])
        idx_f = sb("idx_f", [P, TPB, TOPK])
        idx = sb("idx", [P, TPB, TOPK], U32)
        hi = sb("hi", [P, 2, BLK], F32R)
        lo = sb("lo", [P, 2, BLK], F32R)
        vout = sb("vout", [P, 2, D])

        p_turn = [ps(f"p_turn{j}", [P, KT, P]) for j in range(2)]
        p_proj = [ps(f"p_proj{j}", [P, BLK]) for j in range(4)]
        p_lg = ps("p_lg", [P, TPB, P])
        p_pos = ps("p_pos", [P, TPB, P])

        weights_in, consts, iotas, blank_ready, blank_out = map(sem, ("weights_in", "consts", "iotas", "blank_ready", "blank_out"))
        x_free, x_in, eps_ready, var_ready, std_ready = map(sem, ("x_free", "x_in", "eps_ready", "var_ready", "std_ready"))
        xn_ready, turned, xnT_ready, xnT_out, logits = map(sem, ("xn_ready", "turned", "xnT_ready", "xnT_out", "logits"))
        top_ready, ex_ready, mask_ready, pos_ready, idx_ready = map(sem, ("top_ready", "ex_ready", "mask_ready", "pos_ready", "idx_ready"))
        sent, proj_done, hi_ready, lo_ready, v_ready = map(sem, ("sent", "proj_done", "hi_ready", "lo_ready", "v_ready"))
        out_slot = [sem(f"out_slot{j}") for j in range(2)]
        v_slot = [sem(f"v_slot{j}") for j in range(2)]
        norm_order, route_order, gate_ready, gate_out = map(sem, ("norm_order", "route_order", "gate_ready", "gate_out"))

        block = ctx.enter_context(nc.Block())

        @block.sync
        def _(sp):
            for n in range(NW):
                sp.dma_start(w[:, n, :, :], w_dram[n].rearrange("(k p) n -> p k n", p=P)).then_inc(weights_in, 16)
            sp.dma_start(wr[:, :, :], wr_dram.rearrange("(k p) n -> p k n", p=P)).then_inc(weights_in, 16)
            with sp.Fori(0, B) as b:
                with sp.Fori(0, BPB) as c:
                    blk = b * BPB + c
                    for n in range(NG):
                        m, ft = n // KT, n % KT
                        for part, stage, ready in ((0, hi, hi_ready), (1, lo, lo_ready)):
                            sp.wait_ge(ready, blk * NG + n + 1)
                            src = stage[:, n % 2, :].bitcast(F32)
                            if m % 2 == 0:
                                dst = qd[bass.ds(b, 1), 4 * ft:4 * ft + 4, bass.ds(c, 1), part * DH:(part + 1) * DH, m // 2, :]
                                dst = dst.rearrange("b h c d t -> (b c h) d t")
                            else:
                                dst = kd[bass.ds(b, 1), 4 * ft:4 * ft + 4, part * DH:(part + 1) * DH, m // 2, bass.ds(c * BLK, BLK)]
                                dst = dst.rearrange("b h d t -> (b h) d t")
                            sp.dma_start(dst, src).then_inc(out_slot[n % 2], 16)
                    for t in range(TPB):
                        sp.wait_ge(v_ready, blk * TPB + t + 1)
                        dst = vd[bass.ds(b, 1), :, :, bass.ds(c * TPB + t, 1), :].rearrange("b h p o d -> p (b o h) d")
                        sp.dma_start(dst, vout[:, t % 2, :].rearrange("p (h d) -> p h d", h=H)).then_inc(v_slot[t % 2], 16)
            sp.wait_ge(gate_ready, NBLK)
            sp.dma_start(gate_d, gate[:, :]).then_inc(gate_out, 16)
            for j in range(2):
                sp.wait_ge(out_slot[j], NBLK * NG // 2 * 32 + 32)
                sp.wait_ge(v_slot[j], NBLK * TPB // 2 * 16 + 16)
            sp.wait_ge(gate_out, 16)

        @block.gpsimd
        def _(pool):
            pool.memset(ident[:, :], 0.0).then_inc(iotas, 1)
            pool.memset(before[:, :], 1.0).then_inc(iotas, 1)
            pool.memset(ones[:, :], 1.0).then_inc(consts, 1)
            pool.memset(blank[:, :], 0.0).then_inc(iotas, 1)
            pool.iota(iota_i[:, :], pattern=[[1, E]], base=0, channel_multiplier=0).then_inc(iotas, 1)
            for a in range(0, P, CAP):
                pool.wait_ge(iotas, 4 + a // CAP)
                pool.wait_ge(consts, 1)
                pool.iota(dummy_i[a:a + CAP, :], pattern=[[0, 1]], base=T, channel_multiplier=1).then_inc(iotas, 1)
            pool.wait_ge(iotas, 6)
            pool.iota(tok_i[:, :], pattern=[[P, TPB]], base=0, channel_multiplier=1).then_inc(iotas, 1)
            pool.wait_ge(iotas, 7)
            pool.affine_select(out=ident[:, :], in_=ident[:, :], compare_op=ALU.not_equal, fill=1.0, base=0,
                               pattern=[[-1, P]], channel_multiplier=1).then_inc(consts, 1)
            pool.affine_select(out=before[:, :], in_=before[:, :], compare_op=ALU.is_ge, fill=0.0, base=-1,
                               pattern=[[1, P]], channel_multiplier=-1).then_inc(consts, 1)
            pool.tensor_copy(blank[:, C_TOK:C_TOK + 1], dummy_i[:, :]).then_inc(blank_ready, 1)
            pool.tensor_copy(e_iota[:, :], iota_i[:, :]).then_inc(iotas, 1)
            pool.tensor_copy(tok_f[:, :], tok_i[:, :]).then_inc(consts, 1)
            pool.wait_ge(iotas, 8)
            pool.tensor_scalar(e_slot[:, :], e_iota[:, :], float(CAP), None, ALU.mult).then_inc(consts, 1)
            pool.wait_ge(blank_ready, 1)
            for j in range(E * CAP // P):
                pool.dma_start(xe[j * P:(j + 1) * P, :], blank[:, :]).then_inc(blank_out, 16)
            pool.wait_ge(blank_out, E * CAP // P * 16)
            with pool.Fori(0, NBLK) as i:
                pool.wait_ge(x_free, i + 1)
                pool.dma_start(xin[:, :, :], x[bass.ds(i * BLK, BLK), :].rearrange("(t p) d -> p t d", p=P)).then_inc(x_in, 16)
                pool.wait_ge(idx_ready, i + 1)
                stand(pool, passed)
                for t in range(TPB):
                    for k in range(TOPK):
                        pool.indirect_dma_start(xe, bass.IndirectOffsetOnAxis(idx[:, t, k:k + 1], 0), xn[:, t, :], None,
                                                bounds_check=E * CAP - 1, oob_is_err=False).then_inc(sent, 16)
            pool.wait_ge(sent, NBLK * TPB * TOPK * 16)

        @block.tensor
        def _(pe):
            pe.wait_ge(consts, 5)
            pe.wait_ge(weights_in, (NW + 1) * 16)
            with pe.Fori(0, NBLK) as i:
                pe.wait_ge(xn_ready, i + 1)
                for t in range(TPB):
                    if t >= 2:
                        pe.wait_ge(xnT_ready, i * TPB + t - 1)
                    for k in range(KT):
                        last = pe.transpose(p_turn[t % 2][:, k, :], xn[:, t, k * P:(k + 1) * P], ident[:, :])
                    last.then_inc(turned, 1)
                pe.wait_ge(xnT_ready, i * TPB + TPB)
                for t in range(TPB):
                    for k in range(KT):
                        last = pe.matmul(p_lg[:, t, 0:E + 1], xnT[:, k, t * P:(t + 1) * P], wr[:, k, :],
                                         start=(k == 0), stop=(k == KT - 1))
                last.then_inc(logits, 1)
                for n in range(NGV):
                    if n >= 4:
                        pe.wait_ge(lo_ready, i * NG + n - 3)
                    for k in range(KT):
                        if n < NG:
                            lhs, rhs = w[:, n // KT, k, (n % KT) * P:(n % KT + 1) * P], xnT[:, k, :]
                        else:
                            lhs, rhs = xnT[:, k, (n - NG) * P:(n - NG + 1) * P], w[:, 4, k, :]
                        last = pe.matmul(p_proj[n % 4][:, :], lhs, rhs, start=(k == 0), stop=(k == KT - 1))
                    last.then_inc(proj_done, 1)
                    if n == 5:
                        pe.wait_ge(mask_ready, i + 1)
                        for t in range(TPB):
                            pe.matmul(p_pos[:, t, 0:E], before[:, :], mask[:, t, :], start=True, stop=False)
                            for t2 in range(t):
                                pe.matmul(p_pos[:, t, 0:E], ones[:, :], mask[:, t2, :], start=False, stop=False)
                            last = pe.matmul(p_pos[:, t, 0:E], ones[:, :], carry_b[:, :], start=False, stop=True)
                        last.then_inc(pos_ready, 1)

        @block.scalar
        def _(act):
            act.sem_inc(out_slot[0], 32)
            act.sem_inc(out_slot[1], 32)
            act.sem_inc(v_slot[0], 16)
            act.sem_inc(v_slot[1], 16)
            act.sem_inc(xnT_out, 16)

            def std_of(i):
                act.wait_ge(var_ready, i + 1)
                act.activation(std[:, :], mv[:, :, 1], ACT.Sqrt, bias=eps[:, 0:1]).then_inc(std_ready, 1)

            def a_block(i, more):
                for t in range(TPB):
                    act.wait_ge(turned, i * TPB + t + 1)
                    if t == 0:
                        act.wait_ge(xnT_out, i * 16 + 16)
                    act.activation(xnT[:, :, t * P:(t + 1) * P], p_turn[t % 2][:, :, :], ACT.Copy).then_inc(xnT_ready, 1)
                act.wait_ge(xnT_ready, i * TPB + TPB)
                act.dma_start(xnt_d[bass.ds(i, 1), :, :, :].rearrange("o p k t -> (o p) k t"), xnT[:, :, :]).then_inc(xnT_out, 16)
                act.wait_ge(top_ready, i + 1)
                for t in range(TPB):
                    act.activation(ex[:, t, :], top[:, t, 0:TOPK], ACT.Exp, bias=ntop[:, t:t + 1],
                                   accum_out=exs[:, t:t + 1]).then_inc(ex_ready, 1)
                act.activation(se_e[:, :], lg[:, :, E], ACT.Exp, scale=-1.0).then_inc(ex_ready, 1)
                for n in range(NGV):
                    act.wait_ge(proj_done, i * NGV + n + 1)
                    if n < NG:
                        act.wait_ge(out_slot[n % 2], (i * (NG // 2) + n // 2) * 32 + 32)
                        act.activation(hi[:, n % 2, :], p_proj[n % 4][:, :], ACT.Copy,
                                       scale=Q_SCALE if (n // KT) % 2 == 0 else 1.0).then_inc(hi_ready, 1)
                    else:
                        v = n - NG
                        act.wait_ge(v_slot[v % 2], (i * (TPB // 2) + v // 2) * 16 + 16)
                        act.activation(vout[:, v % 2, :], p_proj[n % 4][:, :], ACT.Copy).then_inc(v_ready, 1)
                    if more and n == 9:
                        std_of(i + 1)

            act.wait_ge(eps_ready, 2)
            std_of(0)
            with act.Fori(0, NBLK - 1) as i:
                a_block(i, True)
            a_block(NBLK - 1, False)
            act.wait_ge(xnT_out, NBLK * 16 + 16)

        @block.vector
        def _(dve):
            dve.memset(eps[:, :], LN_EPS).then_inc(eps_ready, 1)
            dve.memset(carry[:, :], 0.0).then_inc(eps_ready, 1)
            dve.memset(xn[:, :, D:ROW], 0.0).then_inc(eps_ready, 1)
            dve.memset(carry_b[:, :], 0.0).then_inc(x_free, 1)
            dve.wait_ge(consts, 5)
            nlink = linker(dve, norm_order, TPB + 1)
            rlink = linker(dve, route_order, 17)

            def norm(i):
                dve.wait_ge(x_in, i * 16 + 16)
                for t in range(TPB):
                    nlink(dve.bn_stats(stats[:, t, :], xin[:, t, :]), i)
                stand(dve, passed)
                for t in range(TPB):
                    last = dve.bn_aggr(mv[:, t, :], stats[:, t, :])
                last.then_inc(var_ready, 1)
                dve.wait_ge(std_ready, i + 1)
                nlink(dve.reciprocal(rstd[:, :], std[:, :]), i)
                dve.wait_ge(var_ready, i + 1)
                if not isinstance(i, int) or i:
                    dve.wait_ge(sent, i * (TPB * TOPK * 16))
                for t in range(TPB):
                    last = dve.tensor_scalar(xn[:, t, 0:D], xin[:, t, :], mv[:, t, 0:1], rstd[:, t:t + 1], ALU.subtract, ALU.mult)
                last.then_inc(xn_ready, 1)
                dve.tensor_copy(xn[:, :, C_TOK], tok_f[:, :]).then_inc(x_free, 1)

            def route(i):
                dve.wait_ge(logits, i + 1)
                rlink(dve.tensor_copy(lg[:, :, :], p_lg[:, :, 0:E + 1]), i)
                stand(dve, passed)
                for t in range(TPB):
                    last = dve.max(top[:, t, :], lg[:, t, 0:E])
                rlink(last, i)
                stand(dve, passed)
                for t in range(TPB):
                    last = dve.max_index(topi[:, t, :], top[:, t, :], lg[:, t, 0:E])
                rlink(last, i)
                dve.tensor_scalar(ntop[:, :], top[:, :, 0], -1.0, None, ALU.mult).then_inc(top_ready, 1)
                rlink(dve.tensor_copy(xn[:, :, C_E:C_E + TOPK], topi[:, :, 0:TOPK]), i)
                rlink(dve.tensor_tensor(eq[:, :, :, :],
                                        e_iota[:, :].rearrange("p (a b e) -> p a b e", a=1, b=1).broadcast_to([P, TPB, TOPK, E]),
                                        xn[:, :, C_E:C_E + TOPK].rearrange("p t (k a) -> p t k a", a=1).broadcast_to([P, TPB, TOPK, E]),
                                        ALU.is_equal), i)
                with nc.allow_low_precision(reason="0 or 1"):
                    rlink(dve.tensor_reduce(mask[:, :, :], eq[:, :, :, :].rearrange("p t k e -> p t e k"), AX_X, ALU.add), i)
                dve.tensor_reduce(blk_n[:, :], mask[:, :, :].rearrange("p t e -> p e t"), AX_X, ALU.add).then_inc(mask_ready, 1)
                dve.wait_ge(ex_ready, i * (TPB + 1) + TPB + 1)
                rlink(dve.reciprocal(exr[:, :], exs[:, :]), i)
                rlink(dve.tensor_tensor(xn[:, :, C_W:C_W + TOPK], ex[:, :, :],
                                        exr[:, :].rearrange("p (t a) -> p t a", a=1).broadcast_to([P, TPB, TOPK]), ALU.mult), i)
                rlink(dve.tensor_scalar(se_e[:, :], se_e[:, :], 1.0, None, ALU.add), i)
                dve.reciprocal(gate[:, bass.ds(i * TPB, TPB)], se_e[:, :]).then_inc(gate_ready, 1)

            def place(i):
                dve.wait_ge(pos_ready, i + 1)
                rlink(dve.tensor_scalar(over[:, :, :], p_pos[:, :, 0:E], CAP - 0.5, FAR, ALU.is_gt, ALU.mult), i)
                rlink(dve.tensor_tensor(slot[:, :, :], p_pos[:, :, 0:E],
                                        e_slot[:, :].rearrange("p (a e) -> p a e", a=1).broadcast_to([P, TPB, E]), ALU.add), i)
                dve.wait_ge(mask_ready, i + 1)
                rlink(dve.tensor_tensor(carry[:, :], carry[:, :], blk_n[:, :], ALU.add), i)
                rlink(dve.tensor_tensor(slot[:, :, :], slot[:, :, :], over[:, :, :], ALU.add), i)
                rlink(dve.tensor_tensor(picked[:, :, :, :], eq[:, :, :, :],
                                        slot[:, :, :].rearrange("p t (a e) -> p t a e", a=1).broadcast_to([P, TPB, TOPK, E]),
                                        ALU.mult), i)
                rlink(dve.tensor_reduce(idx_f[:, :, :], picked[:, :, :, :], AX_X, ALU.add), i)
                rlink(dve.tensor_copy(carry_b[:, :], carry[:, :]), i)
                dve.tensor_copy(idx[:, :, :], idx_f[:, :, :]).then_inc(idx_ready, 1)
                rlink(dve.tensor_scalar(tok_f[:, :], tok_f[:, :], float(BLK), None, ALU.add), i)

            def split(i, ns):
                for n in ns:
                    dve.wait_ge(hi_ready, i * NG + n + 1)
                    dve.scalar_tensor_tensor(lo[:, n % 2, :], p_proj[n % 4][:, :], Q_SCALE if (n // KT) % 2 == 0 else 1.0,
                                             hi[:, n % 2, :].bitcast(F32), ALU.mult, ALU.subtract).then_inc(lo_ready, 1)

            def v_block(i, more):
                route(i)
                split(i, range(0, 6))
                place(i)
                split(i, range(6, 9))
                if more:
                    norm(i + 1)
                split(i, range(9, NG))

            norm(0)
            with dve.Fori(0, NBLK - 1) as i:
                v_block(i, True)
            v_block(NBLK - 1, False)
            dve.wait_ge(idx_ready, NBLK)


HALF = S // 2
TILES = ITERS * TPB
SLOT = [0, 1, 2] * 5 + [1]
PRIOR = [max([m for m in range(j) if SLOT[m] == SLOT[j]], default=None) for j in range(16)]
PRIOR = [max(m for m in range(16) if SLOT[m] == SLOT[j]) - 16 if p is None else p for j, p in enumerate(PRIOR)]


def attend(nc, qd, kd, vd, lam, od):
    with ExitStack() as ctx:
        sb, ps, sem = allocators(nc, ctx, "attend")
        passed = sem("passed")
        q = [sb(f"q{t}", [P, 2, P], F32R) for t in range(TPB)]
        k = sb("k", [P, 2, 2, S], F32R)
        v = sb("v", [P, S // P, DH])
        p1 = [sb(f"p1_{t}", [P, S]) for t in range(TPB)]
        p2 = [sb(f"p2_{t}", [P, S]) for t in range(TPB)]
        aT = [sb(f"aT{t}", [P, S // P, 2 * P]) for t in range(2)]
        ident = sb("ident2", [P, P])
        fold = sb("fold", [P, DH])
        lamb = sb("lamb", [P, H])
        rowmax = sb("rowmax", [P, TPB, 4])
        nmax = sb("nmax", [P, TPB, 2])
        sums = sb("sums", [P, TPB, 4])
        total = sb("total", [P, TPB, 2])
        recip = sb("recip", [P, TPB, 2])
        coef1 = sb("coef1", [P, 1])
        coef = sb("coef", [P, 1])
        keep = sb("keep", [P, 2])
        o_sb = sb("o_sb", [P, 2 * P])
        o_out = [sb(f"o_out{j}", [P, 2, DH]) for j in range(2)]
        p_s = [ps(f"p_s{j}", [P, HALF]) for j in range(3)]
        p_t = ps("p_t", [P, TPB, P])
        p_o = ps("p_o", [P, 512])

        lam_in, consts2, iotas2, k_in, v_in = map(sem, ("lam_in", "consts2", "iotas2", "k_in", "v_in"))
        q_in = [sem(f"q_in{t}") for t in range(TPB)]
        scores, maxed, nmaxed, expd, summed, recipd = map(sem, ("scores", "maxed", "nmaxed", "expd", "summed", "recipd"))
        scaled, turned2, read_dve, read_act = map(sem, ("scaled", "turned2", "read_dve", "read_act"))
        av_done, o_read, folded, o_ready, coefs, kept = map(sem, ("av_done", "o_read", "folded", "o_ready", "coefs", "kept"))
        o_slot = [sem(f"o_slot{j}") for j in range(2)]
        block = ctx.enter_context(nc.Block())

        @block.sync
        def _(sp):
            def loads(i, new_head=None, v_head=None, out=True):
                for t in range(TPB):
                    if not isinstance(i, int) or i:
                        sp.wait_ge(scores, i * 16 - 16 + 4 * t + 4)
                    if t == 0 and new_head is not None:
                        for part in range(2):
                            for dup in range(2):
                                r = part * 64 + dup * DH
                                sp.dma_start(k[r:r + DH, bass.ds(new_head % 2, 1), :, :].bitcast(F32).rearrange("p o m t -> p (o m) t"),
                                             kd[bass.ds(new_head, 1), part * DH:(part + 1) * DH, :, :].rearrange("o p m t -> (o p) m t"))\
                                  .then_inc(k_in, 16)
                    for dup in range(2):
                        sp.dma_start(q[t][dup * 64:dup * 64 + 64, :, :].bitcast(F32),
                                     qd[bass.ds(i, 1), :, :, t * P:(t + 1) * P].rearrange("o p m t -> (o p) m t")).then_inc(q_in[t], 16)
                    if t == 2 and v_head is not None:
                        if not isinstance(v_head, int) or v_head:
                            sp.wait_ge(av_done, v_head * (S // P // 2))
                        sp.dma_start(v[:, :, :], vd[bass.ds(v_head, 1), :, :, :].rearrange("o p t d -> (o p) t d")).then_inc(v_in, 16)
                    if t % 2 and out:
                        results(i - 2, t // 2)

            def results(i, j):
                sp.wait_ge(o_ready, i * 2 + j + 2)
                sp.dma_start(od[bass.ds(i, 1), :, 2 * j:2 * j + 2, :].rearrange("o p t d -> (o p) t d"), o_out[j][:, :, :])\
                  .then_inc(o_slot[j], 16)

            sp.dma_start(lamb[:, :], lam.broadcast_to([P, H])).then_inc(lam_in, 16)
            loads(0, new_head=0, v_head=0, out=False)
            loads(1, out=False)
            with sp.Fori(2, BPB) as i:
                loads(i)
            with sp.Fori(1, HEADS) as g:
                loads(g * BPB, new_head=g)
                loads(g * BPB + 1, v_head=g)
                with sp.Fori(2, BPB) as c:
                    loads(g * BPB + c)
            for i in (ITERS - 2, ITERS - 1):
                for j in range(2):
                    results(i, j)
            for j in range(2):
                sp.wait_ge(o_slot[j], ITERS * 16 + 16)

        @block.tensor
        def _(pe):
            def half(i, t, n):
                j = 4 * t + n
                if n == 0:
                    pe.wait_ge(q_in[t], i * 32 + 32)
                if not isinstance(i, int) or PRIOR[j] >= 0:
                    pe.wait_ge(expd, i * 16 + PRIOR[j] + 1)
                kb = (i // BPB) % 2
                for c in range(2):
                    at = (n % 2) * HALF + c * 512
                    last = pe.matmul(p_s[SLOT[j]][:, c * 512:(c + 1) * 512], q[t][:, n // 2, :],
                                     k[:, bass.ds(kb, 1), n // 2, at:at + 512].rearrange("p o t -> p (o t)"), start=True, stop=True)
                last.then_inc(scores, 1)

            def turn(i, t, n):
                if n % 2 == 0:
                    pe.wait_ge(scaled, (i * 4 + t) * 2 + n // 2 + 1)
                if n == 0:
                    if not isinstance(i, int) or i or t:
                        pe.wait_ge(read_act, (i * 4 + t) * 2)
                else:
                    pe.wait_ge(read_act if n == 2 else read_dve, (i * 4 + t) * 2 + (1 if n < 3 else 2))
                for c in range(4):
                    at = (4 * n + c) * P
                    pe.matmul(p_t[:, c, :], p1[t][:, at:at + P], ident[:, :], start=True, stop=False, is_transpose=True)
                    last = pe.matmul(p_t[:, c, :], p2[t][:, at:at + P], ident[:, :], start=False, stop=True, is_transpose=True)
                last.then_inc(turned2, 1)

            def av(i, j, n):
                if n == 0:
                    pe.wait_ge(o_ready, i * 2 + j + 1)
                    pe.wait_ge(v_in, (i // BPB) * 16 + 16)
                    pe.wait_ge(read_act, (i * 4 + 2 * j) * 2 + 4)
                    pe.wait_ge(read_dve, (i * 4 + 2 * j) * 2 + 4)
                for c in range(4):
                    last = pe.matmul(p_o[c * DH:(c + 1) * DH, 0:2 * P], v[:, 4 * n + c, :], aT[j][:, 4 * n + c, :],
                                     start=(n == 0), stop=(n == 3), tile_position=(0, c * DH))
                if n == 3:
                    last.then_inc(av_done, 1)

            def fold_o(i, j):
                pe.wait_ge(o_read, i * 2 + j + 1)
                for c in range(2):
                    last = pe.matmul(p_o[:, 256 + c * DH:256 + (c + 1) * DH], o_sb[:, c * P:(c + 1) * P], fold[:, :], start=True, stop=True)
                last.then_inc(folded, 1)

            def step(i, t, here=True):
                past = not isinstance(i, int) or i > 0
                for n in range(4):
                    if here:
                        half(i, t, n)
                    if t % 2 == 0 and past:
                        av(i - 1, t // 2, n)
                    if t % 2 and past and n == 1:
                        fold_o(i - 1, t // 2)
                    if t >= 2 and here:
                        turn(i, t - 2, n)
                    elif t < 2 and past:
                        turn(i - 1, t + 2, n)

            pe.wait_ge(consts2, 2)
            pe.wait_ge(k_in, 64)
            for t in range(TPB):
                step(0, t)
            with pe.Fori(1, ITERS) as i:
                pe.wait_ge(k_in, (i // BPB) * 64 + 64)
                for t in range(TPB):
                    step(i, t)
            for t in range(TPB):
                step(ITERS, t, here=False)

        @block.scalar
        def _(act):
            def read(i, t, n):
                act.wait_ge(turned2, (i * 4 + t) * 4 + n + 1)
                act.activation(aT[t // 2][:, 4 * n:4 * n + 4, (t % 2) * P:(t % 2 + 1) * P], p_t[:, :, :], ACT.Copy).then_inc(read_act, 1)

            def exp(i, t, n):
                m = n // 2
                if n % 2 == 0:
                    act.wait_ge(nmaxed, (i * 4 + t) * 2 + m + 1)
                    if m == 0 and (not isinstance(i, int) or i):
                        act.wait_ge(turned2, (i * 4 + t) * 4 - 12)
                dst = p1[t] if m == 0 else p2[t]
                at = (n % 2) * HALF
                act.activation(dst[:, at:at + HALF], p_s[SLOT[4 * t + n]][:, :], ACT.Exp, bias=nmax[:, t, m:m + 1],
                               accum_out=sums[:, t, n:n + 1]).then_inc(expd, 1)

            def step(i, t, here=True):
                past = not isinstance(i, int) or i > 0
                ti, tt = (i, t - 2) if t >= 2 else (i - 1, t + 2)
                turns = (t >= 2 and here) or (t < 2 and past)
                if t % 2 and past:
                    act.wait_ge(av_done, (i - 1) * 2 + t // 2 + 1)
                    act.activation(o_sb[:, :], p_o[:, 0:2 * P], ACT.Copy).then_inc(o_read, 1)
                if here:
                    exp(i, t, 0)
                if turns:
                    read(ti, tt, 1)
                if here:
                    exp(i, t, 1)
                    exp(i, t, 2)
                if turns:
                    read(ti, tt, 3)
                if here:
                    exp(i, t, 3)

            for t in range(TPB):
                step(0, t)
            with act.Fori(1, ITERS) as i:
                for t in range(TPB):
                    step(i, t)
            for t in range(TPB):
                step(ITERS, t, here=False)

        @block.vector
        def _(dve):
            def row_max(i, t, n):
                dve.wait_ge(scores, i * 16 + 4 * t + n + 1)
                dve.tensor_reduce(rowmax[:, t, n:n + 1], p_s[SLOT[4 * t + n]][:, :], AX_X, ALU.max).then_inc(maxed, 1)

            def neg_max(i, t, m):
                dve.wait_ge(maxed, i * 16 + 4 * t + 2 * m + 2)
                dve.tensor_reduce(nmax[:, t, m:m + 1], rowmax[:, t, 2 * m:2 * m + 2], AX_X, ALU.max, negate=True).then_inc(nmaxed, 1)

            def read(i, t, n):
                dve.wait_ge(turned2, (i * 4 + t) * 4 + n + 1)
                dve.tensor_copy(aT[t // 2][:, 4 * n:4 * n + 4, (t % 2) * P:(t % 2 + 1) * P], p_t[:, :, :]).then_inc(read_dve, 1)

            def reciprocals(i, t):
                dve.wait_ge(summed, i * 4 + t + 1)
                dve.reciprocal(recip[:, t, :], total[:, t, :]).then_inc(recipd, 1)

            def step(i, t, here=True):
                past = not isinstance(i, int) or i > 0
                ti, tt = (i, t - 2) if t >= 2 else (i - 1, t + 2)
                turns = (t >= 2 and here) or (t < 2 and past)
                if here:
                    row_max(i, t, 0)
                if turns:
                    read(ti, tt, 0)
                if here:
                    row_max(i, t, 1)
                    neg_max(i, t, 0)
                if t % 2 and past:
                    j = t // 2
                    dve.wait_ge(folded, (i - 1) * 2 + j + 1)
                    dve.wait_ge(o_slot[j], i * 16)
                    dve.tensor_tensor(o_out[j][:, :, :], p_o[:, 256:256 + 2 * DH].rearrange("p (c d) -> p c d", c=2),
                                      keep[:, :].rearrange("p (c a) -> p c a", a=1).broadcast_to([P, 2, DH]), ALU.mult)\
                       .then_inc(o_ready, 1)
                if t and here:
                    reciprocals(i, t - 1)
                elif t == 0 and past:
                    reciprocals(i - 1, TPB - 1)
                if t % 2 == 0 and past:
                    if not here:
                        dve.wait_ge(o_ready, (i - 1) * 2 + t // 2 + 1)
                    dve.wait_ge(recipd, i * 4 + t - 2)
                    dve.tensor_copy(keep[:, :], recip[:, t:t + 2, 0]).then_inc(kept, 1)
                    dve.wait_ge(kept, (i - 1) * 2 + t // 2 + 1)
                if here:
                    row_max(i, t, 2)
                if turns:
                    read(ti, tt, 2)
                if here:
                    row_max(i, t, 3)
                    neg_max(i, t, 1)

            for j in range(2):
                dve.sem_inc(o_slot[j], 16)
            dve.sem_inc(o_ready, 1)
            for t in range(TPB):
                step(0, t)
            with dve.Fori(1, ITERS) as i:
                for t in range(TPB):
                    step(i, t)
            for t in range(TPB):
                step(ITERS, t, here=False)

        @block.gpsimd
        def _(pool):
            pool.memset(ident[:, :], 0.0).then_inc(iotas2, 1)
            pool.memset(fold[:, :], 0.0).then_inc(iotas2, 1)
            pool.wait_ge(iotas2, 2)
            pool.affine_select(out=ident[:, :], in_=ident[:, :], compare_op=ALU.not_equal, fill=1.0, base=0,
                               pattern=[[-1, P]], channel_multiplier=1).then_inc(consts2, 1)
            for a in range(4):
                pool.affine_select(out=fold[:, :], in_=fold[:, :], compare_op=ALU.not_equal, fill=1.0, base=-a * DH,
                                   pattern=[[-1, DH]], channel_multiplier=1).then_inc(consts2 if a == 3 else iotas2, 1)
                if a < 3:
                    pool.wait_ge(iotas2, 3 + a)
            pool.wait_ge(lam_in, 16)

            def scale(i, h, t):
                n = i * 4 + t
                pool.wait_ge(expd, i * 16 + 4 * t + 4)
                pool.tensor_tensor(total[:, t, :], sums[:, t, :].rearrange("p (m h) -> p m h", m=2)[:, :, 0],
                                   sums[:, t, :].rearrange("p (m h) -> p m h", m=2)[:, :, 1], ALU.add).then_inc(summed, 1)
                pool.wait_ge(summed, n + 1)
                stand(pool, passed)
                pool.tensor_tensor(coef1[:, :], total[:, t, 0:1], lamb[:, bass.ds(h, 1)], ALU.mult).then_inc(coefs, 1)
                pool.wait_ge(coefs, 2 * n + 1)
                pool.wait_ge(recipd, n + 1)
                stand(pool, passed)
                pool.tensor_scalar(coef[:, :], coef1[:, :], recip[:, t, 1:2], -1.0, ALU.mult, ALU.mult).then_inc(coefs, 1)
                pool.wait_ge(coefs, 2 * n + 2)
                for c in range(2):
                    part = p2[t][:, c * HALF:(c + 1) * HALF]
                    pool.tensor_tensor(part, part, coef[:, 0:1].broadcast_to([P, HALF]), ALU.mult).then_inc(scaled, 1)

            with pool.Fori(0, B) as b:
                with pool.Fori(0, H) as h:
                    with pool.Fori(0, BPB) as c:
                        for t in range(TPB):
                            scale((b * H + h) * BPB + c, h, t)


def shared(nc, xnt_d, gate_d, wsg, wsu, wsd, acc):
    with ExitStack() as ctx:
        sb, ps, sem = allocators(nc, ctx, "shared")
        wg = sb("wg", [P, KT, FS])
        wu = sb("wu", [P, KT, FS])
        wd = sb("wd", [P, FSN, D])
        gate = sb("gate3", [P, NBLK * TPB])
        gcol = sb("gcol", [P, TPB])
        xT = sb("xT", [P, KT, BLK])
        th = sb("th", [P, 2, BLK])
        gg = sb("gg", [P, 2, BLK])
        hT = sb("hT", [P, FSN, BLK])
        y = sb("y", [P, 2, D])
        zero = sb("zero", [CAP, D])
        p_g = [ps(f"p_g{j}", [P, BLK]) for j in range(2)]
        p_u = [ps(f"p_u{j}", [P, BLK]) for j in range(2)]
        p_y = [ps(f"p_y{j}", [P, D]) for j in range(2)]
        wg_in, wu_in, wd_in, gate_in, x_in, zeroed, zero_out = map(
            sem, ("wg_in", "wu_in", "wd_in", "gate_in", "xT_in", "zeroed", "zero_out"))
        g_done, u_done, th_ready, gg_ready, h_ready, y_done, gcol_ready, y_ready = map(
            sem, ("g_done", "u_done", "th_ready", "gg_ready", "h_ready", "y_done", "gcol_ready", "y_ready"))
        y_slot = [sem(f"y_slot{j}") for j in range(2)]
        block = ctx.enter_context(nc.Block())

        @block.sync
        def _(sp):
            def load(i):
                sp.dma_start(xT[:, :, :], xnt_d[bass.ds(i, 1), :, :, :].rearrange("o p k t -> (o p) k t")).then_inc(x_in, 16)

            def store(i):
                for t in range(TPB):
                    sp.wait_ge(y_ready, i * TPB + t + 3)
                    sp.dma_start(acc[bass.ds(i * BLK + t * P, P), :], y[:, t % 2, :]).then_inc(y_slot[t % 2], 16)

            sp.dma_start(wg[:, :, :], wsg.rearrange("(k p) n -> p k n", p=P)).then_inc(wg_in, 16)
            sp.dma_start(wu[:, :, :], wsu.rearrange("(k p) n -> p k n", p=P)).then_inc(wu_in, 16)
            load(0)
            sp.dma_start(wd[:, :, :], wsd.rearrange("(k p) n -> p k n", p=P)).then_inc(wd_in, 16)
            sp.dma_start(gate[:, :], gate_d).then_inc(gate_in, 16)
            sp.wait_ge(zeroed, 1)
            sp.dma_start(acc[T:T + CAP, :], zero[:, :]).then_inc(zero_out, 16)
            with sp.Fori(1, NBLK) as i:
                sp.wait_ge(u_done, i * FSN)
                load(i)
                store(i - 1)
            store(NBLK - 1)
            sp.wait_ge(zero_out, 16)
            for j in range(2):
                sp.wait_ge(y_slot[j], NBLK * TPB // 2 * 16 + 16)

        @block.gpsimd
        def _(pool):
            pool.memset(zero[:, :], 0.0).then_inc(zeroed, 1)

        @block.tensor
        def _(pe):
            pe.wait_ge(wg_in, 16)
            pe.wait_ge(wu_in, 16)
            pe.wait_ge(wd_in, 16)
            with pe.Fori(0, NBLK) as i:
                pe.wait_ge(x_in, i * 16 + 16)
                for f in range(FSN):
                    if f >= 2:
                        pe.wait_ge(h_ready, i * FSN + f - 1)
                    for w, p, done in ((wg, p_g, g_done), (wu, p_u, u_done)):
                        for k in range(KT):
                            last = pe.matmul(p[f % 2][:, :], w[:, k, f * P:(f + 1) * P], xT[:, k, :], start=(k == 0), stop=(k == KT - 1))
                        last.then_inc(done, 1)
                pe.wait_ge(h_ready, i * FSN + FSN)
                for t in range(TPB):
                    pe.wait_ge(y_ready, i * TPB + t + 1)
                    for f in range(FSN):
                        last = pe.matmul(p_y[t % 2][:, :], hT[:, f, t * P:(t + 1) * P], wd[:, f, :], start=(f == 0), stop=(f == FSN - 1))
                    last.then_inc(y_done, 1)

        @block.scalar
        def _(act):
            act.sem_inc(y_ready, 2)
            act.sem_inc(y_slot[0], 16)
            act.sem_inc(y_slot[1], 16)
            with act.Fori(0, NBLK) as i:
                for f in range(FSN):
                    act.wait_ge(g_done, i * FSN + f + 1)
                    act.activation(th[:, f % 2, :], p_g[f % 2][:, :], ACT.Tanh, scale=0.5).then_inc(th_ready, 1)
                act.wait_ge(gcol_ready, i + 1)
                for t in range(TPB):
                    act.wait_ge(y_done, i * TPB + t + 1)
                    act.wait_ge(y_slot[t % 2], (i * 2 + t // 2) * 16 + 16)
                    act.activation(y[:, t % 2, :], p_y[t % 2][:, :], ACT.Copy, scale=gcol[:, t:t + 1]).then_inc(y_ready, 1)

        @block.vector
        def _(dve):
            dve.wait_ge(gate_in, 16)
            with dve.Fori(0, NBLK) as i:
                for f in range(FSN):
                    dve.wait_ge(th_ready, i * FSN + f + 1)
                    dve.scalar_tensor_tensor(gg[:, f % 2, :], th[:, f % 2, :], 1.0, p_g[f % 2][:, :], ALU.add, ALU.mult)\
                       .then_inc(gg_ready, 1)
                    dve.wait_ge(gg_ready, i * FSN + f + 1)
                    dve.wait_ge(u_done, i * FSN + f + 1)
                    dve.scalar_tensor_tensor(hT[:, f, :], gg[:, f % 2, :], 0.5, p_u[f % 2][:, :], ALU.mult, ALU.mult)\
                       .then_inc(h_ready, 1)
                dve.wait_ge(y_ready, i * TPB + 2)
                dve.tensor_copy(gcol[:, :], gate[:, bass.ds(i * TPB, TPB)]).then_inc(gcol_ready, 1)


def experts(nc, xe, wge, wue, wde, acc):
    with ExitStack() as ctx:
        sb, ps, sem = allocators(nc, ctx, "experts")
        passed = sem("passed")
        wg = [sb(f"ewg{j}", [P, KT, F]) for j in range(2)]
        wu = [sb(f"ewu{j}", [P, KT, F]) for j in range(2)]
        wd = [sb(f"ewd{j}", [FT, FN, D]) for j in range(2)]
        rows = [sb(f"rows{j}", [CAP, ROW]) for j in range(2)]
        xT = sb("exT", [P, KT, CAP])
        th = sb("eth", [FT, FN, CAP])
        gg = sb("egg", [FT, FN, CAP])
        hT = sb("ehT", [FT, FN, CAP])
        ye = [sb(f"ye{j}", [CAP, D]) for j in range(2)]
        tok = [sb(f"tok{j}", [CAP, 1], U32) for j in range(2)]
        mine = sb("mine", [CAP, TOPK])
        weight = [sb(f"weight{j}", [CAP, 1]) for j in range(2)]
        now = sb("now", [CAP, 1])
        ident = sb("ident4", [P, P])
        p_x = ps("p_x", [P, KT, P])
        p_g = ps("ep_g", [FT, FN, CAP])
        p_u = ps("ep_u", [FT, FN, CAP])
        p_y = ps("ep_y", [CAP, D])
        g_in = [sem(f"g_in{j}") for j in range(2)]
        consts4, iota4, xturned, xT_ready, g_done, u_done, th_ready, gg_ready, h_ready = map(
            sem, ("consts4", "iota4", "xturned", "exT_ready", "eg_done", "eu_done", "eth_ready", "egg_ready", "eh_ready"))
        y_done, ye_ready, w_ready, added, tok_ready = map(sem, ("ey_done", "ye_ready", "w_ready", "added", "tok_ready"))
        block = ctx.enter_context(nc.Block())

        @block.sync
        def _(sp):
            with sp.Fori(0, E // 2) as r:
                for j in range(2):
                    e = r * 2 + j
                    sp.wait_ge(ye_ready, e + 1)
                    sp.dma_start(rows[j][:, :], xe[bass.ds(e * CAP, CAP), :]).then_inc(g_in[j], 16)
                    sp.dma_start(wg[j][:, :, :], wge[bass.ds(e, 1), :, :].rearrange("o (k p) f -> p (o k) f", p=P)).then_inc(g_in[j], 16)
                    sp.dma_start(wu[j][:, :, :], wue[bass.ds(e, 1), :, :].rearrange("o (k p) f -> p (o k) f", p=P)).then_inc(g_in[j], 16)
                    sp.dma_start(wd[j][:, :, :], wde[bass.ds(e, 1), :, :].rearrange("o (k p) f -> p (o k) f", p=FT)).then_inc(g_in[j], 16)

        @block.gpsimd
        def _(pool):
            pool.memset(ident[:, :], 0.0).then_inc(iota4, 1)
            pool.wait_ge(iota4, 1)
            pool.affine_select(out=ident[:, :], in_=ident[:, :], compare_op=ALU.not_equal, fill=1.0, base=0,
                               pattern=[[-1, P]], channel_multiplier=1).then_inc(consts4, 1)

            def add(r):
                for j in range(2):
                    e = r * 2 + j
                    pool.wait_ge(ye_ready, e + 3)
                    if not isinstance(e, int) or e:
                        pool.wait_ge(added, e * 16)
                    stand(pool, passed)
                    pool.indirect_dma_start(acc, bass.IndirectOffsetOnAxis(tok[j][:, :], 0), ye[j][:, :], None,
                                            bounds_check=T + CAP - 1, oob_is_err=True, compute_op=ALU.add).then_inc(added, 16)

            add(0)
            with pool.Fori(1, E // 2) as r:
                add(r)
            pool.wait_ge(added, E * 16)

        @block.tensor
        def _(pe):
            pe.wait_ge(consts4, 1)
            with pe.Fori(0, E // 2) as r:
                for j in range(2):
                    e = r * 2 + j
                    pe.wait_ge(g_in[j], r * 64 + 64)
                    stand(pe, passed)
                    for k in range(KT):
                        last = pe.transpose(p_x[:, k, 0:CAP], rows[j][:, k * P:(k + 1) * P], ident[0:CAP, 0:CAP])
                    last.then_inc(xturned, 1)
                    pe.wait_ge(xT_ready, e + 1)
                    for w, p, done in ((wg, p_g, g_done), (wu, p_u, u_done)):
                        for f in range(FN):
                            for k in range(KT):
                                last = pe.matmul(p[:, f, :], w[j][:, k, f * FT:(f + 1) * FT], xT[:, k, :], start=(k == 0), stop=(k == KT - 1))
                        last.then_inc(done, 1)
                    pe.wait_ge(h_ready, e + 1)
                    for f in range(FN):
                        last = pe.matmul(p_y[:, :], hT[:, f, :], wd[j][:, f, :], start=(f == 0), stop=(f == FN - 1))
                    last.then_inc(y_done, 1)

        @block.scalar
        def _(act):
            act.sem_inc(ye_ready, 2)

            def pair(r):
                for j in range(2):
                    e = r * 2 + j
                    act.wait_ge(xturned, e + 1)
                    act.activation(xT[:, :, :], p_x[:, :, 0:CAP], ACT.Copy).then_inc(xT_ready, 1)
                    act.wait_ge(g_done, e + 1)
                    act.activation(th[:, :, :], p_g[:, :, :], ACT.Tanh, scale=0.5).then_inc(th_ready, 1)
                    act.wait_ge(y_done, e + 1)
                    act.wait_ge(tok_ready, e + 2)
                    if not isinstance(r, int):
                        act.wait_ge(added, e * 16 - 16)
                    act.activation(ye[j][:, :], p_y[:, :], ACT.Copy, scale=weight[j][:, 0:1]).then_inc(ye_ready, 1)

            pair(0)
            with act.Fori(1, E // 2) as r:
                pair(r)

        @block.vector
        def _(dve):
            dve.memset(now[:, :], 0.0).then_inc(tok_ready, 1)

            def pair(r):
                for j in range(2):
                    e = r * 2 + j
                    dve.wait_ge(g_in[j], r * 64 + 64)
                    dve.wait_ge(tok_ready, e + 1)
                    dve.wait_ge(ye_ready, e + 1)
                    if not isinstance(r, int):
                        dve.wait_ge(added, e * 16 - 16)
                    dve.scalar_tensor_tensor(mine[:, :], rows[j][:, C_E:C_E + TOPK], now[:, 0:1], rows[j][:, C_W:C_W + TOPK],
                                             ALU.is_equal, ALU.mult, accum_out=weight[j][:, 0:1]).then_inc(w_ready, 1)
                    dve.wait_ge(w_ready, e * 2 + 1)
                    dve.tensor_copy(tok[j][:, :], rows[j][:, C_TOK:C_TOK + 1]).then_inc(w_ready, 1)
                    dve.wait_ge(w_ready, e * 2 + 2)
                    dve.tensor_scalar(now[:, :], now[:, :], 1.0, None, ALU.add).then_inc(tok_ready, 1)
                    dve.wait_ge(th_ready, e + 1)
                    dve.scalar_tensor_tensor(gg[:, :, :], th[:, :, :], 1.0, p_g[:, :, :], ALU.add, ALU.mult).then_inc(gg_ready, 1)
                    dve.wait_ge(gg_ready, e + 1)
                    dve.wait_ge(u_done, e + 1)
                    dve.scalar_tensor_tensor(hT[:, :, :], gg[:, :, :], 0.5, p_u[:, :, :], ALU.mult, ALU.mult).then_inc(h_ready, 1)

            pair(0)
            with dve.Fori(1, E // 2) as r:
                pair(r)


def finish(nc, x, od, wo_dram, acc, out):
    with ExitStack() as ctx:
        sb, ps, sem = allocators(nc, ctx, "finish")
        wo = sb("wo", [P, KT, D])
        a = [sb(f"a{j}", [P, TPB, D]) for j in range(2)]
        xs = [sb(f"xs{j}", [P, TPB, D]) for j in range(2)]
        ff = [sb(f"ff{j}", [P, TPB, D]) for j in range(2)]
        aT = [sb(f"oaT{j}", [P, KT, P]) for j in range(2)]
        ident = sb("ident5", [P, P])
        p_t = [ps(f"op_t{j}", [P, KT, P]) for j in range(2)]
        p_y = [ps(f"op_y{j}", [P, D]) for j in range(2)]
        wo_in, consts5, iota5, turned, aT_ready, y_done, xf, done = map(
            sem, ("wo_in", "consts5", "iota5", "oturned", "oaT_ready", "oy_done", "xf", "odone"))
        stored = [sem(f"stored{j}") for j in range(2)]
        blk_in = [sem(f"blk_in{j}") for j in range(2)]
        block = ctx.enter_context(nc.Block())
        LOADS = (TPB + 2) * 16

        @block.sync
        def _(sp):
            sp.dma_start(wo[:, :, :], wo_dram.rearrange("(k p) n -> p k n", p=P)).then_inc(wo_in, 16)
            for j in range(2):
                sp.sem_inc(stored[j], 16)
            with sp.Fori(0, B) as b:
                with sp.Fori(0, BPB // 2) as r:
                    for j in range(2):
                        c = r * 2 + j
                        i = b * BPB + c
                        sp.wait_ge(stored[j], (b * (BPB // 2) + r) * 16 + 16)
                        for t in range(TPB):
                            src = od[bass.ds(b, 1), :, bass.ds(c, 1), :, t, :].rearrange("b h c p d -> p (b c h) d")
                            sp.dma_start(a[j][:, t, :].rearrange("p (h d) -> p h d", h=H), src).then_inc(blk_in[j], 16)
                        sp.dma_start(xs[j][:, :, :], x[bass.ds(i * BLK, BLK), :].rearrange("(t p) d -> p t d", p=P)).then_inc(blk_in[j], 16)
                        sp.dma_start(ff[j][:, :, :], acc[bass.ds(i * BLK, BLK), :].rearrange("(t p) d -> p t d", p=P)).then_inc(blk_in[j], 16)

        @block.gpsimd
        def _(pool):
            pool.memset(ident[:, :], 0.0).then_inc(iota5, 1)
            pool.wait_ge(iota5, 1)
            pool.affine_select(out=ident[:, :], in_=ident[:, :], compare_op=ALU.not_equal, fill=1.0, base=0,
                               pattern=[[-1, P]], channel_multiplier=1).then_inc(consts5, 1)

        @block.tensor
        def _(pe):
            def turn(n, j, t):
                for k in range(KT):
                    last = pe.transpose(p_t[t % 2][:, k, :], a[j][:, t, k * P:(k + 1) * P], ident[:, :])
                last.then_inc(turned, 1)

            pe.wait_ge(consts5, 1)
            pe.wait_ge(wo_in, 16)
            with pe.Fori(0, NBLK // 2) as r:
                for j in range(2):
                    pe.wait_ge(blk_in[j], r * LOADS + LOADS)
                    for t in range(TPB):
                        n = (r * 2 + j) * TPB + t
                        turn(n, j, t)
                        pe.wait_ge(aT_ready, n + 1)
                        pe.wait_ge(done, n + 1)
                        for k in range(KT):
                            last = pe.matmul(p_y[t % 2][:, :], aT[t % 2][:, k, :], wo[:, k, :], start=(k == 0), stop=(k == KT - 1))
                        last.then_inc(y_done, 1)

        @block.scalar
        def _(act):
            with act.Fori(0, NBLK // 2) as r:
                for j in range(2):
                    for t in range(TPB):
                        act.wait_ge(turned, (r * 2 + j) * TPB + t + 1)
                        act.activation(aT[t % 2][:, :, :], p_t[t % 2][:, :, :], ACT.Copy).then_inc(aT_ready, 1)
                    act.wait_ge(done, (r * 2 + j) * TPB + TPB + 2)
                    act.dma_start(out[bass.ds((r * 2 + j) * BLK, BLK), :].rearrange("(t p) d -> p t d", p=P), xs[j][:, :, :]).then_inc(stored[j], 16)
            for j in range(2):
                act.wait_ge(stored[j], NBLK // 2 * 16 + 16)

        @block.vector
        def _(dve):
            dve.sem_inc(done, 2)
            with dve.Fori(0, NBLK // 2) as r:
                for j in range(2):
                    dve.wait_ge(blk_in[j], r * LOADS + LOADS)
                    for t in range(TPB):
                        n = (r * 2 + j) * TPB + t
                        dve.tensor_tensor(xs[j][:, t, :], xs[j][:, t, :], ff[j][:, t, :], ALU.add).then_inc(xf, 1)
                        dve.wait_ge(xf, n + 1)
                        dve.wait_ge(y_done, n + 1)
                        dve.tensor_tensor(xs[j][:, t, :], p_y[t % 2][:, :], xs[j][:, t, :], ALU.add).then_inc(done, 1)


def build(nc, x, wq1, wk1, wq2, wk2, wv, wo, lam, wr, wge, wue, wde, wsg, wsu, wsd, out):
    def dram(name, shape):
        return nc.dram_tensor(name, shape, F32, kind="Internal").ap()

    xe = dram("xe", [E * CAP, ROW])
    xnt_d = dram("xnt_d", [NBLK, P, KT, BLK])
    qd = dram("qd", [B, H, BPB, 2 * DH, 2, BLK])
    kd = dram("kd", [B, H, 2 * DH, 2, S])
    vd = dram("vd", [B, H, P, S // P, DH])
    gate_d = dram("gate_d", [P, NBLK * TPB])
    od = dram("od", [B, H, BPB, P, TPB, DH])
    acc = dram("acc", [T + CAP, D])
    project(nc, x, (wq1, wk1, wq2, wk2, wv), wr, xe, xnt_d, qd, kd, vd, gate_d)
    attend(nc, qd.rearrange("b h c p m t -> (b h c) p m t"), kd.rearrange("b h p m t -> (b h) p m t"),
           vd.rearrange("b h p t d -> (b h) p t d"), lam, od.rearrange("b h c p t d -> (b h c) p t d"))
    shared(nc, xnt_d, gate_d, wsg, wsu, wsd, acc)
    experts(nc, xe, wge, wue, wde, acc)
    finish(nc, x, od, wo, acc, out)


def kernel(**inputs):
    import numpy as np
    import concourse.bacc as bacc
    from concourse.bass_utils import run_bass_kernel_spmd

    a = {n: np.asarray(v) for n, v in inputs.items()}
    turned = [np.ascontiguousarray(a[f"L0_attn_{n}_w"].T) for n in ("q1", "k1", "q2", "k2", "v", "o")]
    arrays = {
        "x": np.ascontiguousarray(a["L0_attn_x"].reshape(T, D)),
        "wq1": turned[0], "wk1": turned[1], "wq2": turned[2], "wk2": turned[3], "wv": turned[4], "wo": turned[5],
        "lam": np.ascontiguousarray(a["L0_attn_lambda_param"].reshape(1, H)),
        "wr": np.ascontiguousarray(np.concatenate([a["L0_ffn_Wr"], a["L0_ffn_Wse"]], axis=1)),
        "wge": a["L0_ffn_Wg"], "wue": a["L0_ffn_Wu"], "wde": a["L0_ffn_Wd"],
        "wsg": a["L0_ffn_Wsg"], "wsu": a["L0_ffn_Wsu"], "wsd": a["L0_ffn_Wsd"],
    }
    nc = bacc.Bacc("TRN2", target_bir_lowering=False, num_devices=1)
    args = [nc.dram_tensor(f"in_{n}", v.shape, F32, kind="ExternalInput").ap() for n, v in arrays.items()]
    out = nc.dram_tensor("out", [T, D], F32, kind="ExternalOutput").ap()
    build(nc, *args, out)
    r = run_bass_kernel_spmd(nc, [{f"in_{n}": v for n, v in arrays.items()}], core_ids=[0])
    return np.asarray(r.results[0]["out"]).reshape(B, S, D)
```

```python
from contextlib import ExitStack

import concourse.bass as bass
from concourse import mybir

ALU = mybir.AluOpType
ACT = mybir.ActivationFunctionType
F32 = mybir.dt.float32
F32R = mybir.dt.float32r
BF16 = mybir.dt.bfloat16
I32 = mybir.dt.int32
U32 = mybir.dt.uint32
AX_X = mybir.AxisListType.X

P = 128
B, S, D = 2, 2048, 512
H, DH = 16, 32
T = B * S
KT = D // P
BLK = 512
NBLK = T // BLK
BPB = S // BLK
TPB = BLK // P
HEADS = B * H
ITERS = HEADS * BPB
E, TOPK, CAP = 32, 4, 64
F, FS = 352, 1408
FN = -(-F // P)
F0 = [min(f * P, F - P) for f in range(FN)]
FPAD = FN * P - F
FSN = FS // P
ROW = D + 16
C_TOK, C_W, C_E = D, D + 1, D + 1 + TOPK
LN_EPS = 1e-5
FAR = 1.0e6
Q_SCALE = float(DH) ** -0.5
NG = 4 * KT
NGV = NG + TPB


def allocators(nc, ctx, stage):
    def sb(name, shape, dt=F32):
        return ctx.enter_context(nc.sbuf_tensor(f"{stage}_{name}", shape, dt))

    def ps(name, shape, dt=F32):
        return ctx.enter_context(nc.psum_tensor(f"{stage}_{name}", shape, dt))

    def sem(name):
        return ctx.enter_context(nc.semaphore(f"{stage}_{name}"))

    return sb, ps, sem


def stand(eng, passed):
    eng.sem_inc(passed, 1)


def linker(eng, order, per_round):
    done = [0]

    def link(ins, i):
        done[0] = done[0] % per_round + 1
        ins.then_inc(order, 1)
        eng.wait_ge(order, i * per_round + done[0])

    return link


def project(nc, x, w_dram, wr_dram, xe, xnt_d, qd, kd, vd, gate_d):
    with ExitStack() as ctx:
        sb, ps, sem = allocators(nc, ctx, "project")
        passed = sem("passed")
        NW = 5
        w = sb("w", [P, NW, KT, D])
        wr = sb("wr", [P, KT, E + 1])
        xin = sb("xin", [P, TPB, D])
        xn = sb("xn", [P, TPB, ROW])
        xnT = sb("xnT", [P, KT, BLK])
        ident = sb("ident", [P, P])
        before = sb("before", [P, P], BF16)
        ones = sb("ones", [P, P], BF16)
        e_iota = sb("e_iota", [P, E])
        e_slot = sb("e_slot", [P, E])
        iota_i = sb("iota_i", [P, E], I32)
        tok_i = sb("tok_i", [P, TPB], I32)
        tok_f = sb("tok_f", [P, TPB])
        blank = sb("blank", [P, ROW])
        dummy_i = sb("dummy_i", [P, 1], I32)
        stats = sb("stats", [P, TPB, 6])
        mv = sb("mv", [P, TPB, 2])
        std = sb("std", [P, TPB])
        rstd = sb("rstd", [P, TPB])
        eps = sb("eps", [P, 1])
        lg = sb("lg", [P, TPB, E + 1])
        top = sb("top", [P, TPB, 8])
        topi = sb("topi", [P, TPB, 8], U32)
        ntop = sb("ntop", [P, TPB])
        ex = sb("ex", [P, TPB, TOPK])
        exs = sb("exs", [P, TPB])
        exr = sb("exr", [P, TPB])
        se_e = sb("se_e", [P, TPB])
        gate = sb("gate", [P, NBLK * TPB])
        eq = sb("eq", [P, TPB, TOPK, E])
        mask = sb("mask", [P, TPB, E], BF16)
        carry = sb("carry", [P, E])
        carry_b = sb("carry_b", [P, E], BF16)
        blk_n = sb("blk_n", [P, E])
        over = sb("over", [P, TPB, E])
        slot = sb("slot", [P, TPB, E])
        picked = sb("picked", [P, TPB, TOPK, E])
        idx_f = sb("idx_f", [P, TPB, TOPK])
        idx = sb("idx", [P, TPB, TOPK], U32)
        hi = sb("hi", [P, 2, BLK], F32R)
        lo = sb("lo", [P, 2, BLK], F32R)
        vout = sb("vout", [P, 2, D])

        p_turn = [ps(f"p_turn{j}", [P, KT, P]) for j in range(2)]
        p_proj = [ps(f"p_proj{j}", [P, BLK]) for j in range(4)]
        p_lg = ps("p_lg", [P, TPB, P])
        p_pos = ps("p_pos", [P, TPB, P])

        weights_in, consts, iotas, blank_ready, blank_out = map(sem, ("weights_in", "consts", "iotas", "blank_ready", "blank_out"))
        x_free, x_in, eps_ready, var_ready, std_ready = map(sem, ("x_free", "x_in", "eps_ready", "var_ready", "std_ready"))
        xn_ready, turned, xnT_ready, xnT_out, logits = map(sem, ("xn_ready", "turned", "xnT_ready", "xnT_out", "logits"))
        top_ready, ex_ready, mask_ready, pos_ready, idx_ready = map(sem, ("top_ready", "ex_ready", "mask_ready", "pos_ready", "idx_ready"))
        sent, proj_done, hi_ready, lo_ready, v_ready = map(sem, ("sent", "proj_done", "hi_ready", "lo_ready", "v_ready"))
        out_slot = [sem(f"out_slot{j}") for j in range(2)]
        v_slot = [sem(f"v_slot{j}") for j in range(2)]
        norm_order, route_order, gate_ready, gate_out = map(sem, ("norm_order", "route_order", "gate_ready", "gate_out"))

        block = ctx.enter_context(nc.Block())

        @block.sync
        def _(sp):
            for n in range(NW):
                sp.dma_start(w[:, n, :, :], w_dram[n].rearrange("(k p) n -> p k n", p=P)).then_inc(weights_in, 16)
            sp.dma_start(wr[:, :, :], wr_dram.rearrange("(k p) n -> p k n", p=P)).then_inc(weights_in, 16)
            with sp.Fori(0, B) as b:
                with sp.Fori(0, BPB) as c:
                    blk = b * BPB + c
                    for n in range(NG):
                        m, ft = n // KT, n % KT
                        for part, stage, ready in ((0, hi, hi_ready), (1, lo, lo_ready)):
                            sp.wait_ge(ready, blk * NG + n + 1)
                            src = stage[:, n % 2, :].bitcast(F32)
                            if m % 2 == 0:
                                dst = qd[bass.ds(b, 1), 4 * ft:4 * ft + 4, bass.ds(c, 1), part * DH:(part + 1) * DH, m // 2, :]
                                dst = dst.rearrange("b h c d t -> (b c h) d t")
                            else:
                                dst = kd[bass.ds(b, 1), 4 * ft:4 * ft + 4, part * DH:(part + 1) * DH, m // 2, bass.ds(c * BLK, BLK)]
                                dst = dst.rearrange("b h d t -> (b h) d t")
                            sp.dma_start(dst, src).then_inc(out_slot[n % 2], 16)
                    for t in range(TPB):
                        sp.wait_ge(v_ready, blk * TPB + t + 1)
                        dst = vd[bass.ds(b, 1), :, :, bass.ds(c * TPB + t, 1), :].rearrange("b h p o d -> p (b o h) d")
                        sp.dma_start(dst, vout[:, t % 2, :].rearrange("p (h d) -> p h d", h=H)).then_inc(v_slot[t % 2], 16)
            sp.wait_ge(gate_ready, NBLK)
            sp.dma_start(gate_d, gate[:, :]).then_inc(gate_out, 16)
            for j in range(2):
                sp.wait_ge(out_slot[j], NBLK * NG // 2 * 32 + 32)
                sp.wait_ge(v_slot[j], NBLK * TPB // 2 * 16 + 16)
            sp.wait_ge(gate_out, 16)

        @block.gpsimd
        def _(pool):
            pool.memset(ident[:, :], 0.0).then_inc(iotas, 1)
            pool.memset(before[:, :], 1.0).then_inc(iotas, 1)
            pool.memset(ones[:, :], 1.0).then_inc(consts, 1)
            pool.memset(blank[:, :], 0.0).then_inc(iotas, 1)
            pool.iota(iota_i[:, :], pattern=[[1, E]], base=0, channel_multiplier=0).then_inc(iotas, 1)
            for a in range(0, P, CAP):
                pool.wait_ge(iotas, 4 + a // CAP)
                pool.wait_ge(consts, 1)
                pool.iota(dummy_i[a:a + CAP, :], pattern=[[0, 1]], base=T, channel_multiplier=1).then_inc(iotas, 1)
            pool.wait_ge(iotas, 6)
            pool.iota(tok_i[:, :], pattern=[[P, TPB]], base=0, channel_multiplier=1).then_inc(iotas, 1)
            pool.wait_ge(iotas, 7)
            pool.affine_select(out=ident[:, :], in_=ident[:, :], compare_op=ALU.not_equal, fill=1.0, base=0,
                               pattern=[[-1, P]], channel_multiplier=1).then_inc(consts, 1)
            pool.affine_select(out=before[:, :], in_=before[:, :], compare_op=ALU.is_ge, fill=0.0, base=-1,
                               pattern=[[1, P]], channel_multiplier=-1).then_inc(consts, 1)
            pool.tensor_copy(blank[:, C_TOK:C_TOK + 1], dummy_i[:, :]).then_inc(blank_ready, 1)
            pool.tensor_copy(e_iota[:, :], iota_i[:, :]).then_inc(iotas, 1)
            pool.tensor_copy(tok_f[:, :], tok_i[:, :]).then_inc(consts, 1)
            pool.wait_ge(iotas, 8)
            pool.tensor_scalar(e_slot[:, :], e_iota[:, :], float(CAP), None, ALU.mult).then_inc(consts, 1)
            pool.wait_ge(blank_ready, 1)
            for j in range(E * CAP // P):
                pool.dma_start(xe[j * P:(j + 1) * P, :], blank[:, :]).then_inc(blank_out, 16)
            pool.wait_ge(blank_out, E * CAP // P * 16)
            with pool.Fori(0, NBLK) as i:
                pool.wait_ge(x_free, i + 1)
                pool.dma_start(xin[:, :, :], x[bass.ds(i * BLK, BLK), :].rearrange("(t p) d -> p t d", p=P)).then_inc(x_in, 16)
                pool.wait_ge(idx_ready, i + 1)
                stand(pool, passed)
                for t in range(TPB):
                    for k in range(TOPK):
                        pool.indirect_dma_start(xe, bass.IndirectOffsetOnAxis(idx[:, t, k:k + 1], 0), xn[:, t, :], None,
                                                bounds_check=E * CAP - 1, oob_is_err=False).then_inc(sent, 16)
            pool.wait_ge(sent, NBLK * TPB * TOPK * 16)

        @block.tensor
        def _(pe):
            pe.wait_ge(consts, 5)
            pe.wait_ge(weights_in, (NW + 1) * 16)
            with pe.Fori(0, NBLK) as i:
                pe.wait_ge(xn_ready, i + 1)
                for t in range(TPB):
                    if t >= 2:
                        pe.wait_ge(xnT_ready, i * TPB + t - 1)
                    for k in range(KT):
                        last = pe.transpose(p_turn[t % 2][:, k, :], xn[:, t, k * P:(k + 1) * P], ident[:, :])
                    last.then_inc(turned, 1)
                pe.wait_ge(xnT_ready, i * TPB + TPB)
                for t in range(TPB):
                    for k in range(KT):
                        last = pe.matmul(p_lg[:, t, 0:E + 1], xnT[:, k, t * P:(t + 1) * P], wr[:, k, :],
                                         start=(k == 0), stop=(k == KT - 1))
                last.then_inc(logits, 1)
                for n in range(NGV):
                    if n >= 4:
                        pe.wait_ge(lo_ready, i * NG + n - 3)
                    for k in range(KT):
                        if n < NG:
                            lhs, rhs = w[:, n // KT, k, (n % KT) * P:(n % KT + 1) * P], xnT[:, k, :]
                        else:
                            lhs, rhs = xnT[:, k, (n - NG) * P:(n - NG + 1) * P], w[:, 4, k, :]
                        last = pe.matmul(p_proj[n % 4][:, :], lhs, rhs, start=(k == 0), stop=(k == KT - 1))
                    last.then_inc(proj_done, 1)
                    if n == 5:
                        pe.wait_ge(mask_ready, i + 1)
                        for t in range(TPB):
                            pe.matmul(p_pos[:, t, 0:E], before[:, :], mask[:, t, :], start=True, stop=False)
                            for t2 in range(t):
                                pe.matmul(p_pos[:, t, 0:E], ones[:, :], mask[:, t2, :], start=False, stop=False)
                            last = pe.matmul(p_pos[:, t, 0:E], ones[:, :], carry_b[:, :], start=False, stop=True)
                        last.then_inc(pos_ready, 1)

        @block.scalar
        def _(act):
            act.sem_inc(out_slot[0], 32)
            act.sem_inc(out_slot[1], 32)
            act.sem_inc(v_slot[0], 16)
            act.sem_inc(v_slot[1], 16)
            act.sem_inc(xnT_out, 16)

            def std_of(i):
                act.wait_ge(var_ready, i + 1)
                act.activation(std[:, :], mv[:, :, 1], ACT.Sqrt, bias=eps[:, 0:1]).then_inc(std_ready, 1)

            def a_block(i, more):
                for t in range(TPB):
                    act.wait_ge(turned, i * TPB + t + 1)
                    if t == 0:
                        act.wait_ge(xnT_out, i * 16 + 16)
                    act.activation(xnT[:, :, t * P:(t + 1) * P], p_turn[t % 2][:, :, :], ACT.Copy).then_inc(xnT_ready, 1)
                act.wait_ge(xnT_ready, i * TPB + TPB)
                act.dma_start(xnt_d[bass.ds(i, 1), :, :, :].rearrange("o p k t -> (o p) k t"), xnT[:, :, :]).then_inc(xnT_out, 16)
                act.wait_ge(top_ready, i + 1)
                for t in range(TPB):
                    act.activation(ex[:, t, :], top[:, t, 0:TOPK], ACT.Exp, bias=ntop[:, t:t + 1],
                                   accum_out=exs[:, t:t + 1]).then_inc(ex_ready, 1)
                act.activation(se_e[:, :], lg[:, :, E], ACT.Exp, scale=-1.0).then_inc(ex_ready, 1)
                for n in range(NGV):
                    act.wait_ge(proj_done, i * NGV + n + 1)
                    if n < NG:
                        act.wait_ge(out_slot[n % 2], (i * (NG // 2) + n // 2) * 32 + 32)
                        act.activation(hi[:, n % 2, :], p_proj[n % 4][:, :], ACT.Copy,
                                       scale=Q_SCALE if (n // KT) % 2 == 0 else 1.0).then_inc(hi_ready, 1)
                    else:
                        v = n - NG
                        act.wait_ge(v_slot[v % 2], (i * (TPB // 2) + v // 2) * 16 + 16)
                        act.activation(vout[:, v % 2, :], p_proj[n % 4][:, :], ACT.Copy).then_inc(v_ready, 1)
                    if more and n == 9:
                        std_of(i + 1)

            act.wait_ge(eps_ready, 2)
            std_of(0)
            with act.Fori(0, NBLK - 1) as i:
                a_block(i, True)
            a_block(NBLK - 1, False)
            act.wait_ge(xnT_out, NBLK * 16 + 16)

        @block.vector
        def _(dve):
            dve.memset(eps[:, :], LN_EPS).then_inc(eps_ready, 1)
            dve.memset(carry[:, :], 0.0).then_inc(eps_ready, 1)
            dve.memset(xn[:, :, D:ROW], 0.0).then_inc(eps_ready, 1)
            dve.memset(carry_b[:, :], 0.0).then_inc(x_free, 1)
            dve.wait_ge(consts, 5)
            nlink = linker(dve, norm_order, TPB + 1)
            rlink = linker(dve, route_order, 17)

            def norm(i):
                dve.wait_ge(x_in, i * 16 + 16)
                for t in range(TPB):
                    nlink(dve.bn_stats(stats[:, t, :], xin[:, t, :]), i)
                stand(dve, passed)
                for t in range(TPB):
                    last = dve.bn_aggr(mv[:, t, :], stats[:, t, :])
                last.then_inc(var_ready, 1)
                dve.wait_ge(std_ready, i + 1)
                nlink(dve.reciprocal(rstd[:, :], std[:, :]), i)
                dve.wait_ge(var_ready, i + 1)
                if not isinstance(i, int) or i:
                    dve.wait_ge(sent, i * (TPB * TOPK * 16))
                for t in range(TPB):
                    last = dve.tensor_scalar(xn[:, t, 0:D], xin[:, t, :], mv[:, t, 0:1], rstd[:, t:t + 1], ALU.subtract, ALU.mult)
                last.then_inc(xn_ready, 1)
                dve.tensor_copy(xn[:, :, C_TOK], tok_f[:, :]).then_inc(x_free, 1)

            def route(i):
                dve.wait_ge(logits, i + 1)
                rlink(dve.tensor_copy(lg[:, :, :], p_lg[:, :, 0:E + 1]), i)
                stand(dve, passed)
                for t in range(TPB):
                    last = dve.max(top[:, t, :], lg[:, t, 0:E])
                rlink(last, i)
                stand(dve, passed)
                for t in range(TPB):
                    last = dve.max_index(topi[:, t, :], top[:, t, :], lg[:, t, 0:E])
                rlink(last, i)
                dve.tensor_scalar(ntop[:, :], top[:, :, 0], -1.0, None, ALU.mult).then_inc(top_ready, 1)
                rlink(dve.tensor_copy(xn[:, :, C_E:C_E + TOPK], topi[:, :, 0:TOPK]), i)
                rlink(dve.tensor_tensor(eq[:, :, :, :],
                                        e_iota[:, :].rearrange("p (a b e) -> p a b e", a=1, b=1).broadcast_to([P, TPB, TOPK, E]),
                                        xn[:, :, C_E:C_E + TOPK].rearrange("p t (k a) -> p t k a", a=1).broadcast_to([P, TPB, TOPK, E]),
                                        ALU.is_equal), i)
                with nc.allow_low_precision(reason="0 or 1"):
                    rlink(dve.tensor_reduce(mask[:, :, :], eq[:, :, :, :].rearrange("p t k e -> p t e k"), AX_X, ALU.add), i)
                dve.tensor_reduce(blk_n[:, :], mask[:, :, :].rearrange("p t e -> p e t"), AX_X, ALU.add).then_inc(mask_ready, 1)
                dve.wait_ge(ex_ready, i * (TPB + 1) + TPB + 1)
                rlink(dve.reciprocal(exr[:, :], exs[:, :]), i)
                rlink(dve.tensor_tensor(xn[:, :, C_W:C_W + TOPK], ex[:, :, :],
                                        exr[:, :].rearrange("p (t a) -> p t a", a=1).broadcast_to([P, TPB, TOPK]), ALU.mult), i)
                rlink(dve.tensor_scalar(se_e[:, :], se_e[:, :], 1.0, None, ALU.add), i)
                dve.reciprocal(gate[:, bass.ds(i * TPB, TPB)], se_e[:, :]).then_inc(gate_ready, 1)

            def place(i):
                dve.wait_ge(pos_ready, i + 1)
                rlink(dve.tensor_scalar(over[:, :, :], p_pos[:, :, 0:E], CAP - 0.5, FAR, ALU.is_gt, ALU.mult), i)
                rlink(dve.tensor_tensor(slot[:, :, :], p_pos[:, :, 0:E],
                                        e_slot[:, :].rearrange("p (a e) -> p a e", a=1).broadcast_to([P, TPB, E]), ALU.add), i)
                dve.wait_ge(mask_ready, i + 1)
                rlink(dve.tensor_tensor(carry[:, :], carry[:, :], blk_n[:, :], ALU.add), i)
                rlink(dve.tensor_tensor(slot[:, :, :], slot[:, :, :], over[:, :, :], ALU.add), i)
                rlink(dve.tensor_tensor(picked[:, :, :, :], eq[:, :, :, :],
                                        slot[:, :, :].rearrange("p t (a e) -> p t a e", a=1).broadcast_to([P, TPB, TOPK, E]),
                                        ALU.mult), i)
                rlink(dve.tensor_reduce(idx_f[:, :, :], picked[:, :, :, :], AX_X, ALU.add), i)
                rlink(dve.tensor_copy(carry_b[:, :], carry[:, :]), i)
                dve.tensor_copy(idx[:, :, :], idx_f[:, :, :]).then_inc(idx_ready, 1)
                rlink(dve.tensor_scalar(tok_f[:, :], tok_f[:, :], float(BLK), None, ALU.add), i)

            def split(i, ns):
                for n in ns:
                    dve.wait_ge(hi_ready, i * NG + n + 1)
                    dve.scalar_tensor_tensor(lo[:, n % 2, :], p_proj[n % 4][:, :], Q_SCALE if (n // KT) % 2 == 0 else 1.0,
                                             hi[:, n % 2, :].bitcast(F32), ALU.mult, ALU.subtract).then_inc(lo_ready, 1)

            def v_block(i, more):
                route(i)
                split(i, range(0, 6))
                place(i)
                split(i, range(6, 9))
                if more:
                    norm(i + 1)
                split(i, range(9, NG))

            norm(0)
            with dve.Fori(0, NBLK - 1) as i:
                v_block(i, True)
            v_block(NBLK - 1, False)
            dve.wait_ge(idx_ready, NBLK)


HALF = S // 2
TILES = ITERS * TPB
PAIRS = TILES // 2
HUGE = 3.0e38
TURN, MEET, MET, LEAVE = 3, 5, 6, 7
DVE_READS = [(t, 0) for t in range(0, TPB, 2)]
ACT_READS = [(t, n) for t in range(TPB) for n in range(4) if (t, n) not in DVE_READS]


def tile_of(i, t, back):
    d, place = divmod(t - back, TPB)
    if isinstance(i, int) and not 0 <= i + d < ITERS:
        return None
    return i + d, place


def attend(nc, qd, kd, vd, lam, od):
    with ExitStack() as ctx:
        sb, ps, sem = allocators(nc, ctx, "attend")
        passed = sem("passed")
        q = [sb(f"q{t}", [P, 2, P], F32R) for t in range(TPB)]
        k = sb("k", [P, 2, 2, S], F32R)
        v = sb("v", [P, S // P, DH])
        p = [[sb(f"p{m + 1}_{t}", [P, S]) for m in range(2)] for t in range(TPB)]
        aT = [sb(f"aT{t}", [P, S // P, 2 * P]) for t in range(2)]
        ident = sb("ident", [P, P])
        fold = sb("fold", [P, DH])
        lamb = sb("lamb", [P, H])
        low = sb("low", [P, TPB, 2])
        nmax = sb("nmax", [P, TPB, 2])
        sums = sb("sums", [P, TPB, 2])
        recip = sb("recip", [P, TPB, 2])
        coef1 = sb("coef1", [P, 1])
        coef = sb("coef", [P, 1])
        keep = sb("keep", [P, 2, 2])
        o_sb = sb("o_sb", [P, 2 * P])
        o_out = [sb(f"o_out{j}", [P, 2, DH]) for j in range(2)]
        p_s = [ps(f"p_s{j}", [P, HALF]) for j in range(2)]
        p_t = [ps(f"p_t{j}", [P, TPB, P]) for j in range(2)]
        p_o = ps("p_o", [P, 2 * P])
        p_f = ps("p_f", [P, 2, DH])

        lam_in, consts, iotas, k_in, v_in = map(sem, ("lam_in", "consts", "iotas", "k_in", "v_in"))
        q_in = [sem(f"q_in{t}") for t in range(TPB)]
        scores, lifted, expd, recipd, coefs, scaled = map(sem, ("scores", "lifted", "expd", "recipd", "coefs", "scaled"))
        joined = sem("joined")
        turned, read_dve, read_act, av_done, o_read, folded, o_ready, kept = map(
            sem, ("turned", "read_dve", "read_act", "av_done", "o_read", "folded", "o_ready", "kept"))
        o_slot = [sem(f"o_slot{j}") for j in range(2)]
        block = ctx.enter_context(nc.Block())

        def reads(i, t, n):
            if (t, n) in DVE_READS:
                return read_dve, i * len(DVE_READS) + DVE_READS.index((t, n)) + 1
            return read_act, i * len(ACT_READS) + ACT_READS.index((t, n)) + 1

        def run(eng, step):
            for i in range(2):
                for t in range(TPB):
                    step(i, t)
            with eng.Fori(2, ITERS) as i:
                for t in range(TPB):
                    step(i, t)
            for n in range(LEAVE - 1):
                step(ITERS + n // TPB, n % TPB)

        @block.sync
        def _(sp):
            def loads(i, new_head=None, v_head=None):
                for t in range(TPB):
                    if not isinstance(i, int) or i:
                        sp.wait_ge(scores, i * 16 - 16 + 4 * t + 4)
                    if t == 0 and new_head is not None:
                        for part in range(2):
                            for dup in range(2):
                                r = part * 64 + dup * DH
                                sp.dma_start(k[r:r + DH, bass.ds(new_head % 2, 1), :, :].bitcast(F32).rearrange("p o m t -> p (o m) t"),
                                             kd[bass.ds(new_head, 1), part * DH:(part + 1) * DH, :, :].rearrange("o p m t -> (o p) m t"))\
                                  .then_inc(k_in, 16)
                    for dup in range(2):
                        sp.dma_start(q[t][dup * 64:dup * 64 + 64, :, :].bitcast(F32),
                                     qd[bass.ds(i, 1), :, :, t * P:(t + 1) * P].rearrange("o p m t -> (o p) m t")).then_inc(q_in[t], 16)
                    if t == 3 and v_head is not None:
                        if not isinstance(v_head, int) or v_head:
                            sp.wait_ge(av_done, v_head * (S // P // 2))
                        sp.dma_start(v[:, :, :], vd[bass.ds(v_head, 1), :, :, :].rearrange("o p t d -> (o p) t d")).then_inc(v_in, 16)
                    if t % 2:
                        done = tile_of(i, t, TPB + LEAVE)
                        if done:
                            results(done[0], done[1] // 2)

            def results(i, j):
                sp.wait_ge(o_ready, i * 2 + j + 1)
                sp.dma_start(od[bass.ds(i, 1), :, 2 * j:2 * j + 2, :].rearrange("o p t d -> (o p) t d"), o_out[j][:, :, :])\
                  .then_inc(o_slot[j], 16)

            sp.dma_start(lamb[:, :], lam.broadcast_to([P, H])).then_inc(lam_in, 16)
            loads(0, new_head=0, v_head=0)
            for i in range(1, BPB):
                loads(i)
            with sp.Fori(1, HEADS) as g:
                loads(g * BPB, new_head=g)
                loads(g * BPB + 1, v_head=g)
                with sp.Fori(2, BPB) as c:
                    loads(g * BPB + c)
            for n in range(PAIRS - 5, PAIRS):
                results(n // 2, n % 2)
            for j in range(2):
                sp.wait_ge(o_slot[j], ITERS * 16 + 16)

        @block.tensor
        def _(pe):
            def half(i, t, n):
                if n == 0:
                    pe.wait_ge(q_in[t], i * 32 + 32)
                    if t == 0:
                        pe.wait_ge(k_in, (i // BPB) * 64 + 64)
                if not isinstance(i, int) or i or t or n >= 2:
                    pe.wait_ge(lifted, i * 16 + 4 * t + n - 1)
                for c in range(2):
                    at = (n % 2) * HALF + c * 512
                    last = pe.matmul(p_s[n % 2][:, c * 512:(c + 1) * 512], q[t][:, n // 2, :],
                                     k[:, bass.ds((i // BPB) % 2, 1), n // 2, at:at + 512].rearrange("p o t -> p (o t)"),
                                     start=True, stop=True)
                last.then_inc(scores, 1)

            def turn(i, t, n):
                if n == 0:
                    pe.wait_ge(joined, i * 4 + t + 1)
                elif n < 3:
                    pe.wait_ge(scaled, (i * 4 + t) * 2 + n)
                if n >= 2:
                    pe.wait_ge(*reads(i, t, n - 2))
                elif not isinstance(i, int) or i or t:
                    pe.wait_ge(*reads(*((i, t - 1) if t else (i - 1, TPB - 1)), n + 2))
                for c in range(4):
                    at = (4 * n + c) * P
                    last = pe.matmul(p_t[n % 2][:, c, :], p[t][0][:, at:at + P], ident[:, :], start=True, stop=n < 2,
                                     is_transpose=True)
                    if n >= 2:
                        last = pe.matmul(p_t[n % 2][:, c, :], p[t][1][:, at:at + P], ident[:, :], start=False, stop=True,
                                         is_transpose=True)
                last.then_inc(turned, 1)

            def meet(i, j, n):
                if n == 0:
                    pe.wait_ge(o_read, i * 2 + j + 1)
                    pe.wait_ge(v_in, (i // BPB) * 16 + 16)
                    pe.wait_ge(*reads(i, 2 * j + 1, 3))
                    pe.wait_ge(*reads(i, 2 * j, 0))
                for c in range(4):
                    last = pe.matmul(p_o[c * DH:(c + 1) * DH, :], v[:, 4 * n + c, :], aT[j][:, 4 * n + c, :],
                                     start=(n == 0), stop=(n == 3), tile_position=(0, c * DH))
                if n == 3:
                    last.then_inc(av_done, 1)

            def fold_o(i, j):
                pe.wait_ge(o_read, i * 2 + j + 2)
                if not isinstance(i, int) or i or j:
                    pe.wait_ge(o_ready, i * 2 + j)
                for c in range(2):
                    last = pe.matmul(p_f[:, c, :], o_sb[:, c * P:(c + 1) * P], fold[:, :], start=True, stop=True)
                last.then_inc(folded, 1)

            def step(i, t):
                here, old, meets, met, left = (tile_of(i, t, b) for b in (0, TURN, MEET, MET, LEAVE))
                if here:
                    half(i, t, 0)
                if t % 2 == 0 and met:
                    meet(met[0], met[1] // 2, 2)
                if here:
                    half(i, t, 1)
                if old:
                    turn(*old, 0)
                    turn(*old, 1)
                if here:
                    half(i, t, 2)
                if t % 2 and meets:
                    meet(meets[0], meets[1] // 2, 0)
                    meet(meets[0], meets[1] // 2, 1)
                if t % 2 == 0 and met:
                    meet(met[0], met[1] // 2, 3)
                if old:
                    turn(*old, 2)
                if t % 2 and left:
                    fold_o(left[0], left[1] // 2)
                if here:
                    half(i, t, 3)
                if old:
                    turn(*old, 3)

            pe.wait_ge(consts, 2)
            run(pe, step)

        @block.scalar
        def _(act):
            def read(i, t, n):
                act.wait_ge(turned, (i * 4 + t) * 4 + n + 1)
                act.activation(aT[t // 2][:, 4 * n:4 * n + 4, (t % 2) * P:(t % 2 + 1) * P], p_t[n % 2][:, :, :], ACT.Copy)\
                   .then_inc(read_act, 1)

            def exp(i, t, m):
                act.wait_ge(lifted, (i * 4 + t) * 4 + 2 * m + 2)
                act.activation(p[t][m][:, :], p[t][m][:, :], ACT.Exp, bias=nmax[:, t, m:m + 1], scale=-1.0,
                               accum_out=sums[:, t, m:m + 1]).then_inc(expd, 1)

            def step(i, t):
                here, last, old, met = (tile_of(i, t, b) for b in (0, 1, TURN, MET))
                if last:
                    exp(*last, 1)
                if old:
                    if (old[1], 0) in ACT_READS:
                        read(*old, 0)
                    read(*old, 1)
                if here:
                    exp(i, t, 0)
                if old:
                    read(*old, 2)
                    read(*old, 3)
                if t % 2 == 0 and met:
                    act.wait_ge(av_done, met[0] * 2 + met[1] // 2 + 1)
                    act.activation(o_sb[:, :], p_o[:, :], ACT.Copy).then_inc(o_read, 1)

            act.sem_inc(o_read, 1)
            run(act, step)

        @block.vector
        def _(dve):
            def lift(i, t, n):
                m = n // 2
                dve.wait_ge(scores, i * 16 + 4 * t + n + 1)
                if n == 0 and (not isinstance(i, int) or i):
                    dve.wait_ge(turned, (i * 4 + t) * 4 - 12)
                if n % 2:
                    dve.wait_ge(lifted, i * 16 + 4 * t + n)
                at = (n % 2) * HALF
                dve.tensor_scalar(p[t][m][:, at:at + HALF], p_s[n % 2][:, :], -1.0, low[:, t, m:m + 1] if n % 2 else HUGE,
                                  ALU.mult, ALU.min, accum_out=(nmax if n % 2 else low)[:, t, m:m + 1]).then_inc(lifted, 1)

            def step(i, t):
                here, last, old, met, left = (tile_of(i, t, b) for b in (0, 1, TURN, MEET, LEAVE))
                if here:
                    lift(i, t, 0)
                if old and (old[1], 0) in DVE_READS:
                    dve.wait_ge(turned, (old[0] * 4 + old[1]) * 4 + 1)
                    ot = old[1]
                    dve.tensor_copy(aT[ot // 2][:, 0:4, (ot % 2) * P:(ot % 2 + 1) * P], p_t[0][:, :, :]).then_inc(read_dve, 1)
                if here:
                    lift(i, t, 1)
                if t % 2 and met:
                    j = met[1] // 2
                    if not here:
                        dve.wait_ge(o_ready, met[0] * 2 + j - 1)
                    dve.wait_ge(recipd, met[0] * 4 + 2 * j + 2)
                    dve.tensor_copy(keep[:, j, :], recip[:, 2 * j:2 * j + 2, 0]).then_inc(kept, 1)
                if last:
                    if t % 2 and met:
                        dve.wait_ge(kept, met[0] * 2 + met[1] // 2 + 1)
                    dve.wait_ge(expd, (last[0] * 4 + last[1]) * 2 + 2)
                    dve.reciprocal(recip[:, last[1], :], sums[:, last[1], :]).then_inc(recipd, 1)
                if here:
                    lift(i, t, 2)
                if last:
                    dve.wait_ge(coefs, (last[0] * 4 + last[1]) * 3 + 2)
                    p1, p2 = (p[last[1]][m][:, 0:S // 4] for m in range(2))
                    dve.scalar_tensor_tensor(p1, p2, coef[:, 0:1], p1, ALU.mult, ALU.add).then_inc(joined, 1)
                if t % 2 and left:
                    j = left[1] // 2
                    dve.wait_ge(folded, left[0] * 2 + j + 1)
                    dve.wait_ge(kept, left[0] * 2 + j + 1)
                    dve.wait_ge(o_slot[j], left[0] * 16 + 16)
                    dve.tensor_tensor(o_out[j][:, :, :], p_f[:, :, :],
                                      keep[:, j, :].rearrange("p (c a) -> p c a", a=1).broadcast_to([P, 2, DH]), ALU.mult)\
                       .then_inc(o_ready, 1)
                if here:
                    lift(i, t, 3)

            for j in range(2):
                dve.sem_inc(o_slot[j], 16)
            run(dve, step)

        @block.gpsimd
        def _(pool):
            pool.memset(ident[:, :], 0.0).then_inc(iotas, 1)
            pool.memset(fold[:, :], 0.0).then_inc(iotas, 1)
            pool.wait_ge(iotas, 2)
            pool.affine_select(out=ident[:, :], in_=ident[:, :], compare_op=ALU.not_equal, fill=1.0, base=0,
                               pattern=[[-1, P]], channel_multiplier=1).then_inc(consts, 1)
            for a in range(4):
                pool.affine_select(out=fold[:, :], in_=fold[:, :], compare_op=ALU.not_equal, fill=1.0, base=-a * DH,
                                   pattern=[[-1, DH]], channel_multiplier=1).then_inc(consts if a == 3 else iotas, 1)
                if a < 3:
                    pool.wait_ge(iotas, 3 + a)
            pool.wait_ge(lam_in, 16)
            pool.tensor_scalar(lamb[:, :], lamb[:, :], -1.0, None, ALU.mult).then_inc(iotas, 1)
            pool.wait_ge(iotas, 6)

            def scale(i, h, t):
                n = i * 4 + t
                pool.wait_ge(expd, 2 * n + 2)
                stand(pool, passed)
                pool.tensor_tensor(coef1[:, :], sums[:, t, 0:1], lamb[:, bass.ds(h, 1)], ALU.mult).then_inc(coefs, 1)
                pool.wait_ge(coefs, 3 * n + 1)
                pool.wait_ge(recipd, n + 1)
                pool.tensor_tensor(coef[:, :], coef1[:, :], recip[:, t, 1:2], ALU.mult).then_inc(coefs, 1)
                pool.wait_ge(coefs, 3 * n + 2)
                g1, g23 = slice(S // 4, HALF), slice(HALF, S)
                pool.tensor_tensor(p[t][1][:, g1], p[t][1][:, g1], coef[:, 0:1].broadcast_to([P, S // 4]), ALU.mult).then_inc(coefs, 1)
                pool.wait_ge(coefs, 3 * n + 3)
                pool.tensor_tensor(p[t][0][:, g1], p[t][0][:, g1], p[t][1][:, g1], ALU.add).then_inc(scaled, 1)
                pool.tensor_tensor(p[t][1][:, g23], p[t][1][:, g23], coef[:, 0:1].broadcast_to([P, HALF]), ALU.mult).then_inc(scaled, 1)

            with pool.Fori(0, B) as b:
                with pool.Fori(0, H) as h:
                    with pool.Fori(0, BPB) as c:
                        for t in range(TPB):
                            scale((b * H + h) * BPB + c, h, t)


def shared(nc, xnt_d, gate_d, wsg, wsu, wsd, acc):
    with ExitStack() as ctx:
        sb, ps, sem = allocators(nc, ctx, "shared")
        wg = sb("wg", [P, KT, FS])
        wu = sb("wu", [P, KT, FS])
        wd = sb("wd", [P, FSN, D])
        gate = sb("gate3", [P, NBLK * TPB])
        gcol = sb("gcol", [P, TPB])
        xT = sb("xT", [P, KT, BLK])
        th = sb("th", [P, 2, BLK])
        gg = sb("gg", [P, 2, BLK])
        hT = sb("hT", [P, FSN, BLK])
        y = sb("y", [P, 2, D])
        zero = sb("zero", [CAP, D])
        p_g = [ps(f"p_g{j}", [P, BLK]) for j in range(2)]
        p_u = [ps(f"p_u{j}", [P, BLK]) for j in range(2)]
        p_y = [ps(f"p_y{j}", [P, D]) for j in range(2)]
        wg_in, wu_in, wd_in, gate_in, x_in, zeroed, zero_out = map(
            sem, ("wg_in", "wu_in", "wd_in", "gate_in", "xT_in", "zeroed", "zero_out"))
        g_done, u_done, th_ready, gg_ready, h_ready, y_done, gcol_ready, y_ready = map(
            sem, ("g_done", "u_done", "th_ready", "gg_ready", "h_ready", "y_done", "gcol_ready", "y_ready"))
        y_slot = [sem(f"y_slot{j}") for j in range(2)]
        block = ctx.enter_context(nc.Block())

        @block.sync
        def _(sp):
            def load(i):
                sp.dma_start(xT[:, :, :], xnt_d[bass.ds(i, 1), :, :, :].rearrange("o p k t -> (o p) k t")).then_inc(x_in, 16)

            def store(i):
                for t in range(TPB):
                    sp.wait_ge(y_ready, i * TPB + t + 3)
                    sp.dma_start(acc[bass.ds(i * BLK + t * P, P), :], y[:, t % 2, :]).then_inc(y_slot[t % 2], 16)

            sp.dma_start(wg[:, :, :], wsg.rearrange("(k p) n -> p k n", p=P)).then_inc(wg_in, 16)
            sp.dma_start(wu[:, :, :], wsu.rearrange("(k p) n -> p k n", p=P)).then_inc(wu_in, 16)
            load(0)
            sp.dma_start(wd[:, :, :], wsd.rearrange("(k p) n -> p k n", p=P)).then_inc(wd_in, 16)
            sp.dma_start(gate[:, :], gate_d).then_inc(gate_in, 16)
            sp.wait_ge(zeroed, 1)
            sp.dma_start(acc[T:T + CAP, :], zero[:, :]).then_inc(zero_out, 16)
            with sp.Fori(1, NBLK) as i:
                sp.wait_ge(u_done, i * FSN)
                load(i)
                store(i - 1)
            store(NBLK - 1)
            sp.wait_ge(zero_out, 16)
            for j in range(2):
                sp.wait_ge(y_slot[j], NBLK * TPB // 2 * 16 + 16)

        @block.gpsimd
        def _(pool):
            pool.memset(zero[:, :], 0.0).then_inc(zeroed, 1)

        @block.tensor
        def _(pe):
            pe.wait_ge(wg_in, 16)
            pe.wait_ge(wu_in, 16)
            pe.wait_ge(wd_in, 16)
            with pe.Fori(0, NBLK) as i:
                pe.wait_ge(x_in, i * 16 + 16)
                for f in range(FSN):
                    if f >= 2:
                        pe.wait_ge(h_ready, i * FSN + f - 1)
                    for w, p, done in ((wg, p_g, g_done), (wu, p_u, u_done)):
                        for k in range(KT):
                            last = pe.matmul(p[f % 2][:, :], w[:, k, f * P:(f + 1) * P], xT[:, k, :], start=(k == 0), stop=(k == KT - 1))
                        last.then_inc(done, 1)
                pe.wait_ge(h_ready, i * FSN + FSN)
                for t in range(TPB):
                    pe.wait_ge(y_ready, i * TPB + t + 1)
                    for f in range(FSN):
                        last = pe.matmul(p_y[t % 2][:, :], hT[:, f, t * P:(t + 1) * P], wd[:, f, :], start=(f == 0), stop=(f == FSN - 1))
                    last.then_inc(y_done, 1)

        @block.scalar
        def _(act):
            act.sem_inc(y_ready, 2)
            act.sem_inc(y_slot[0], 16)
            act.sem_inc(y_slot[1], 16)
            with act.Fori(0, NBLK) as i:
                for f in range(FSN):
                    act.wait_ge(g_done, i * FSN + f + 1)
                    act.activation(th[:, f % 2, :], p_g[f % 2][:, :], ACT.Tanh, scale=0.5).then_inc(th_ready, 1)
                act.wait_ge(gcol_ready, i + 1)
                for t in range(TPB):
                    act.wait_ge(y_done, i * TPB + t + 1)
                    act.wait_ge(y_slot[t % 2], (i * 2 + t // 2) * 16 + 16)
                    act.activation(y[:, t % 2, :], p_y[t % 2][:, :], ACT.Copy, scale=gcol[:, t:t + 1]).then_inc(y_ready, 1)

        @block.vector
        def _(dve):
            dve.wait_ge(gate_in, 16)
            with dve.Fori(0, NBLK) as i:
                for f in range(FSN):
                    dve.wait_ge(th_ready, i * FSN + f + 1)
                    dve.scalar_tensor_tensor(gg[:, f % 2, :], th[:, f % 2, :], 1.0, p_g[f % 2][:, :], ALU.add, ALU.mult)\
                       .then_inc(gg_ready, 1)
                    dve.wait_ge(gg_ready, i * FSN + f + 1)
                    dve.wait_ge(u_done, i * FSN + f + 1)
                    dve.scalar_tensor_tensor(hT[:, f, :], gg[:, f % 2, :], 0.5, p_u[f % 2][:, :], ALU.mult, ALU.mult)\
                       .then_inc(h_ready, 1)
                dve.wait_ge(y_ready, i * TPB + 2)
                dve.tensor_copy(gcol[:, :], gate[:, bass.ds(i * TPB, TPB)]).then_inc(gcol_ready, 1)


def experts(nc, xe, wge, wue, wde, acc):
    with ExitStack() as ctx:
        sb, ps, sem = allocators(nc, ctx, "experts")
        passed = sem("passed")
        wg = [sb(f"ewg{j}", [P, KT, F]) for j in range(2)]
        wu = [sb(f"ewu{j}", [P, KT, F]) for j in range(2)]
        wd = [sb(f"ewd{j}", [P, FN, D]) for j in range(2)]
        rows = [sb(f"rows{j}", [CAP, ROW]) for j in range(2)]
        xT = sb("exT", [P, KT, CAP])
        th = sb("eth", [P, FN, CAP])
        gg = sb("egg", [P, FN, CAP])
        hT = [sb(f"ehT{j}", [P, FN, CAP]) for j in range(2)]
        ye = [sb(f"ye{j}", [CAP, D]) for j in range(2)]
        tok = [sb(f"tok{j}", [CAP, 1], U32) for j in range(2)]
        mine = sb("mine", [CAP, TOPK])
        weight = [sb(f"weight{j}", [CAP, 1]) for j in range(2)]
        now = sb("now", [CAP, 1])
        ident = sb("ident4", [P, P])
        p_x = ps("p_x", [P, KT, P])
        p_g = ps("ep_g", [P, FN, CAP])
        p_u = ps("ep_u", [P, FN, CAP])
        p_y = [ps(f"ep_y{j}", [CAP, D]) for j in range(2)]
        rows_in = [sem(f"rows_in{j}") for j in range(2)]
        gu_in = [sem(f"gu_in{j}") for j in range(2)]
        wd_in = [sem(f"wd_in{j}") for j in range(2)]
        consts4, iota4, xturned, xT_ready, g_done, u_done, th_ready, gg_ready, h_ready = map(
            sem, ("consts4", "iota4", "xturned", "exT_ready", "eg_done", "eu_done", "eth_ready", "egg_ready", "eh_ready"))
        y_done, ye_ready, w_ready, added, tok_ready = map(sem, ("ey_done", "ye_ready", "w_ready", "added", "tok_ready"))
        block = ctx.enter_context(nc.Block())

        @block.sync
        def _(sp):
            def load(e, j, first=True):
                if not first:
                    sp.wait_ge(xturned, e - 1)
                    stand(sp, passed)
                    sp.wait_ge(tok_ready, e)
                    stand(sp, passed)
                sp.dma_start(rows[j][:, :], xe[bass.ds(e * CAP, CAP), :]).then_inc(rows_in[j], 16)
                if not first:
                    sp.wait_ge(u_done, e - 1)
                    stand(sp, passed)
                for w, dram in ((wg, wge), (wu, wue)):
                    sp.dma_start(w[j][:, :, :], dram[bass.ds(e, 1), :, :].rearrange("o (k p) f -> p (o k) f", p=P)).then_inc(gu_in[j], 16)

            def load_down(e, j, first=False):
                if not first:
                    sp.wait_ge(y_done, e - 1)
                    stand(sp, passed)
                sp.dma_start(wd[j][:, 0:2, :], wde[bass.ds(e, 1), 0:2 * P, :].rearrange("o (k p) f -> p (o k) f", p=P)).then_inc(wd_in[j], 16)
                sp.dma_start(wd[j][FPAD:P, 2, :], wde[bass.ds(e, 1), 2 * P:F, :].rearrange("o p f -> (o p) f")).then_inc(wd_in[j], 16)

            load(0, 0)
            load_down(0, 0, first=True)
            load(1, 1)
            load_down(1, 1, first=True)
            load(2, 0, first=False)
            with sp.Fori(1, E // 2 - 1) as r:
                load_down(r * 2, 0)
                load(r * 2 + 1, 1, first=False)
                load_down(r * 2 + 1, 1)
                load(r * 2 + 2, 0, first=False)
            load_down(E - 2, 0)
            load(E - 1, 1, first=False)
            load_down(E - 1, 1)

        @block.gpsimd
        def _(pool):
            pool.memset(ident[:, :], 0.0).then_inc(iota4, 1)
            for j in range(2):
                pool.memset(wd[j][0:FPAD, 2, :], 0.0).then_inc(consts4, 1)
            pool.wait_ge(iota4, 1)
            pool.affine_select(out=ident[:, :], in_=ident[:, :], compare_op=ALU.not_equal, fill=1.0, base=0,
                               pattern=[[-1, P]], channel_multiplier=1).then_inc(consts4, 1)

            def add(r):
                for j in range(2):
                    e = r * 2 + j
                    pool.wait_ge(ye_ready, e + 3)
                    if not isinstance(e, int) or e:
                        pool.wait_ge(added, e * 16)
                    stand(pool, passed)
                    pool.indirect_dma_start(acc, bass.IndirectOffsetOnAxis(tok[j][:, :], 0), ye[j][:, :], None,
                                            bounds_check=T + CAP - 1, oob_is_err=True, compute_op=ALU.add).then_inc(added, 16)

            add(0)
            with pool.Fori(1, E // 2) as r:
                add(r)
            pool.wait_ge(added, E * 16)

        @block.tensor
        def _(pe):
            def turn(r, j):
                pe.wait_ge(rows_in[j], r * 16 + 16)
                stand(pe, passed)
                for k in range(KT):
                    last = pe.transpose(p_x[:, k, 0:CAP], rows[j][:, k * P:(k + 1) * P], ident[0:CAP, 0:CAP])
                last.then_inc(xturned, 1)

            def gate_up(r, j):
                e = r * 2 + j
                pe.wait_ge(gu_in[j], r * 32 + 32)
                pe.wait_ge(xT_ready, e + 1)
                if not isinstance(e, int) or e:
                    pe.wait_ge(h_ready, e)
                for w, p, done in ((wg, p_g, g_done), (wu, p_u, u_done)):
                    for f in range(FN):
                        for k in range(KT):
                            last = pe.matmul(p[:, f, :], w[j][:, k, F0[f]:F0[f] + P], xT[:, k, :], start=(k == 0), stop=(k == KT - 1))
                    last.then_inc(done, 1)

            def down(r, j):
                e = r * 2 + j
                pe.wait_ge(wd_in[j], r * 32 + 32)
                pe.wait_ge(h_ready, e + 1)
                pe.wait_ge(ye_ready, e + 1)
                for f in range(FN):
                    last = pe.matmul(p_y[j][:, :], hT[j][:, f, :], wd[j][:, f, :], start=(f == 0), stop=(f == FN - 1))
                last.then_inc(y_done, 1)

            def round_(r, j, first=False, final=False):
                gate_up(r, j)
                if not final:
                    turn(*((r, 1) if j == 0 else (r + 1, 0)))
                if not first:
                    down(*((r, 0) if j else (r - 1, 1)))

            pe.wait_ge(consts4, 3)
            turn(0, 0)
            round_(0, 0, first=True)
            round_(0, 1)
            with pe.Fori(1, E // 2 - 1) as r:
                round_(r, 0)
                round_(r, 1)
            round_(E // 2 - 1, 0)
            round_(E // 2 - 1, 1, final=True)
            down(E // 2 - 1, 1)

        @block.scalar
        def _(act):
            act.sem_inc(ye_ready, 2)

            def copy_x(e):
                act.wait_ge(xturned, e + 1)
                act.activation(xT[:, :, :], p_x[:, :, 0:CAP], ACT.Copy).then_inc(xT_ready, 1)

            def tanh(e):
                act.wait_ge(g_done, e + 1)
                act.activation(th[:, :, :], p_g[:, :, :], ACT.Tanh, scale=0.5).then_inc(th_ready, 1)

            def weigh(e, j):
                act.wait_ge(y_done, e + 1)
                act.wait_ge(tok_ready, e + 2)
                if not isinstance(e, int) or e >= 2:
                    act.wait_ge(added, e * 16 - 16)
                act.activation(ye[j][:, :], p_y[j][:, :], ACT.Copy, scale=weight[j][:, 0:1]).then_inc(ye_ready, 1)

            copy_x(0)
            for e in range(2):
                tanh(e)
                copy_x(e + 1)
                if e:
                    weigh(e - 1, 0)
            with act.Fori(1, E // 2 - 1) as r:
                for j in range(2):
                    e = r * 2 + j
                    tanh(e)
                    copy_x(e + 1)
                    weigh(e - 1, 1 - j)
            tanh(E - 2)
            copy_x(E - 1)
            weigh(E - 3, 1)
            tanh(E - 1)
            weigh(E - 2, 0)
            weigh(E - 1, 1)

        @block.vector
        def _(dve):
            dve.memset(now[:, :], 0.0).then_inc(tok_ready, 1)

            def pair(r):
                for j in range(2):
                    e = r * 2 + j
                    dve.wait_ge(th_ready, e + 1)
                    dve.scalar_tensor_tensor(gg[:, :, :], th[:, :, :], 1.0, p_g[:, :, :], ALU.add, ALU.mult).then_inc(gg_ready, 1)
                    dve.wait_ge(gg_ready, e + 1)
                    dve.wait_ge(u_done, e + 1)
                    dve.scalar_tensor_tensor(hT[j][:, :, :], gg[:, :, :], 0.5, p_u[:, :, :], ALU.mult, ALU.mult).then_inc(h_ready, 1)
                    dve.wait_ge(rows_in[j], r * 16 + 16)
                    dve.wait_ge(tok_ready, e + 1)
                    dve.wait_ge(ye_ready, e + 1)
                    if not isinstance(r, int):
                        dve.wait_ge(added, e * 16 - 16)
                    dve.scalar_tensor_tensor(mine[:, :], rows[j][:, C_E:C_E + TOPK], now[:, 0:1], rows[j][:, C_W:C_W + TOPK],
                                             ALU.is_equal, ALU.mult, accum_out=weight[j][:, 0:1]).then_inc(w_ready, 1)
                    dve.wait_ge(w_ready, e * 2 + 1)
                    dve.tensor_copy(tok[j][:, :], rows[j][:, C_TOK:C_TOK + 1]).then_inc(w_ready, 1)
                    dve.wait_ge(w_ready, e * 2 + 2)
                    dve.tensor_scalar(now[:, :], now[:, :], 1.0, None, ALU.add).then_inc(tok_ready, 1)

            pair(0)
            with dve.Fori(1, E // 2) as r:
                pair(r)


def finish(nc, x, od, wo_dram, acc, out):
    with ExitStack() as ctx:
        sb, ps, sem = allocators(nc, ctx, "finish")
        wo = sb("wo", [P, KT, D])
        a = [sb(f"a{j}", [P, TPB, D]) for j in range(2)]
        xs = [sb(f"xs{j}", [P, TPB, D]) for j in range(2)]
        ff = [sb(f"ff{j}", [P, TPB, D]) for j in range(2)]
        aT = [sb(f"oaT{j}", [P, KT, P]) for j in range(2)]
        ident = sb("ident5", [P, P])
        p_t = [ps(f"op_t{j}", [P, KT, P]) for j in range(2)]
        p_y = [ps(f"op_y{j}", [P, D]) for j in range(2)]
        wo_in, consts5, iota5, turned, aT_ready, y_done, xf, done = map(
            sem, ("wo_in", "consts5", "iota5", "oturned", "oaT_ready", "oy_done", "xf", "odone"))
        stored = [sem(f"stored{j}") for j in range(2)]
        blk_in = [sem(f"blk_in{j}") for j in range(2)]
        block = ctx.enter_context(nc.Block())
        LOADS = (TPB + 2) * 16

        @block.sync
        def _(sp):
            sp.dma_start(wo[:, :, :], wo_dram.rearrange("(k p) n -> p k n", p=P)).then_inc(wo_in, 16)
            for j in range(2):
                sp.sem_inc(stored[j], 16)
            with sp.Fori(0, B) as b:
                with sp.Fori(0, BPB // 2) as r:
                    for j in range(2):
                        c = r * 2 + j
                        i = b * BPB + c
                        sp.wait_ge(stored[j], (b * (BPB // 2) + r) * 16 + 16)
                        for t in range(TPB):
                            src = od[bass.ds(b, 1), :, bass.ds(c, 1), :, t, :].rearrange("b h c p d -> p (b c h) d")
                            sp.dma_start(a[j][:, t, :].rearrange("p (h d) -> p h d", h=H), src).then_inc(blk_in[j], 16)
                        sp.dma_start(xs[j][:, :, :], x[bass.ds(i * BLK, BLK), :].rearrange("(t p) d -> p t d", p=P)).then_inc(blk_in[j], 16)
                        sp.dma_start(ff[j][:, :, :], acc[bass.ds(i * BLK, BLK), :].rearrange("(t p) d -> p t d", p=P)).then_inc(blk_in[j], 16)

        @block.gpsimd
        def _(pool):
            pool.memset(ident[:, :], 0.0).then_inc(iota5, 1)
            pool.wait_ge(iota5, 1)
            pool.affine_select(out=ident[:, :], in_=ident[:, :], compare_op=ALU.not_equal, fill=1.0, base=0,
                               pattern=[[-1, P]], channel_multiplier=1).then_inc(consts5, 1)

        @block.tensor
        def _(pe):
            def turn(n, j, t):
                for k in range(KT):
                    last = pe.transpose(p_t[t % 2][:, k, :], a[j][:, t, k * P:(k + 1) * P], ident[:, :])
                last.then_inc(turned, 1)

            pe.wait_ge(consts5, 1)
            pe.wait_ge(wo_in, 16)
            with pe.Fori(0, NBLK // 2) as r:
                for j in range(2):
                    pe.wait_ge(blk_in[j], r * LOADS + LOADS)
                    for t in range(TPB):
                        n = (r * 2 + j) * TPB + t
                        turn(n, j, t)
                        pe.wait_ge(aT_ready, n + 1)
                        pe.wait_ge(done, n + 1)
                        for k in range(KT):
                            last = pe.matmul(p_y[t % 2][:, :], aT[t % 2][:, k, :], wo[:, k, :], start=(k == 0), stop=(k == KT - 1))
                        last.then_inc(y_done, 1)

        @block.scalar
        def _(act):
            with act.Fori(0, NBLK // 2) as r:
                for j in range(2):
                    for t in range(TPB):
                        act.wait_ge(turned, (r * 2 + j) * TPB + t + 1)
                        act.activation(aT[t % 2][:, :, :], p_t[t % 2][:, :, :], ACT.Copy).then_inc(aT_ready, 1)
                    act.wait_ge(done, (r * 2 + j) * TPB + TPB + 2)
                    act.dma_start(out[bass.ds((r * 2 + j) * BLK, BLK), :].rearrange("(t p) d -> p t d", p=P), xs[j][:, :, :]).then_inc(stored[j], 16)
            for j in range(2):
                act.wait_ge(stored[j], NBLK // 2 * 16 + 16)

        @block.vector
        def _(dve):
            dve.sem_inc(done, 2)
            with dve.Fori(0, NBLK // 2) as r:
                for j in range(2):
                    dve.wait_ge(blk_in[j], r * LOADS + LOADS)
                    for t in range(TPB):
                        n = (r * 2 + j) * TPB + t
                        dve.tensor_tensor(xs[j][:, t, :], xs[j][:, t, :], ff[j][:, t, :], ALU.add).then_inc(xf, 1)
                        dve.wait_ge(xf, n + 1)
                        dve.wait_ge(y_done, n + 1)
                        dve.tensor_tensor(xs[j][:, t, :], p_y[t % 2][:, :], xs[j][:, t, :], ALU.add).then_inc(done, 1)


def build(nc, x, wq1, wk1, wq2, wk2, wv, wo, lam, wr, wge, wue, wde, wsg, wsu, wsd, out):
    def dram(name, shape):
        return nc.dram_tensor(name, shape, F32, kind="Internal").ap()

    xe = dram("xe", [E * CAP, ROW])
    xnt_d = dram("xnt_d", [NBLK, P, KT, BLK])
    qd = dram("qd", [B, H, BPB, 2 * DH, 2, BLK])
    kd = dram("kd", [B, H, 2 * DH, 2, S])
    vd = dram("vd", [B, H, P, S // P, DH])
    gate_d = dram("gate_d", [P, NBLK * TPB])
    od = dram("od", [B, H, BPB, P, TPB, DH])
    acc = dram("acc", [T + CAP, D])
    project(nc, x, (wq1, wk1, wq2, wk2, wv), wr, xe, xnt_d, qd, kd, vd, gate_d)
    attend(nc, qd.rearrange("b h c p m t -> (b h c) p m t"), kd.rearrange("b h p m t -> (b h) p m t"),
           vd.rearrange("b h p t d -> (b h) p t d"), lam, od.rearrange("b h c p t d -> (b h c) p t d"))
    shared(nc, xnt_d, gate_d, wsg, wsu, wsd, acc)
    experts(nc, xe, wge, wue, wde, acc)
    finish(nc, x, od, wo, acc, out)


def kernel(**inputs):
    import numpy as np
    import concourse.bacc as bacc
    from concourse.bass_utils import run_bass_kernel_spmd

    a = {n: np.asarray(v) for n, v in inputs.items()}
    turned = [np.ascontiguousarray(a[f"L0_attn_{n}_w"].T) for n in ("q1", "k1", "q2", "k2", "v", "o")]
    arrays = {
        "x": np.ascontiguousarray(a["L0_attn_x"].reshape(T, D)),
        "wq1": turned[0], "wk1": turned[1], "wq2": turned[2], "wk2": turned[3], "wv": turned[4], "wo": turned[5],
        "lam": np.ascontiguousarray(a["L0_attn_lambda_param"].reshape(1, H)),
        "wr": np.ascontiguousarray(np.concatenate([a["L0_ffn_Wr"], a["L0_ffn_Wse"]], axis=1)),
        "wge": a["L0_ffn_Wg"], "wue": a["L0_ffn_Wu"], "wde": a["L0_ffn_Wd"],
        "wsg": a["L0_ffn_Wsg"], "wsu": a["L0_ffn_Wsu"], "wsd": a["L0_ffn_Wsd"],
    }
    nc = bacc.Bacc("TRN2", target_bir_lowering=False, num_devices=1)
    args = [nc.dram_tensor(f"in_{n}", v.shape, F32, kind="ExternalInput").ap() for n, v in arrays.items()]
    out = nc.dram_tensor("out", [T, D], F32, kind="ExternalOutput").ap()
    build(nc, *args, out)
    r = run_bass_kernel_spmd(nc, [{f"in_{n}": v for n, v in arrays.items()}], core_ids=[0])
    return np.asarray(r.results[0]["out"]).reshape(B, S, D)
```

```python
from contextlib import ExitStack

import concourse.bass as bass
from concourse import mybir

ALU = mybir.AluOpType
ACT = mybir.ActivationFunctionType
F32 = mybir.dt.float32
F32R = mybir.dt.float32r
BF16 = mybir.dt.bfloat16
I32 = mybir.dt.int32
U32 = mybir.dt.uint32
AX_X = mybir.AxisListType.X

P = 128
B, S, D = 2, 2048, 512
H, DH = 16, 32
T = B * S
KT = D // P
BLK = 512
NBLK = T // BLK
BPB = S // BLK
TPB = BLK // P
HEADS = B * H
ITERS = HEADS * BPB
E, TOPK, CAP = 32, 4, 64
F, FS = 352, 1408
FN = -(-F // P)
F0 = [min(f * P, F - P) for f in range(FN)]
FPAD = FN * P - F
ESLOTS = 4
FSN = FS // P
ROW = D + 16
C_TOK, C_W, C_E = D, D + 1, D + 1 + TOPK
LN_EPS = 1e-5
FAR = 1.0e6
Q_SCALE = float(DH) ** -0.5
SBLK = 256
NSB = T // SBLK
TPS = SBLK // P
NG = 4 * KT
NGV = NG + TPB


def allocators(nc, ctx, stage):
    def sb(name, shape, dt=F32):
        return ctx.enter_context(nc.sbuf_tensor(f"{stage}_{name}", shape, dt))

    def ps(name, shape, dt=F32):
        return ctx.enter_context(nc.psum_tensor(f"{stage}_{name}", shape, dt))

    def sem(name):
        return ctx.enter_context(nc.semaphore(f"{stage}_{name}"))

    return sb, ps, sem


def products(pe, out, a, b, first, last):
    pe.matmul(out, a[0], b[0], start=first, stop=False)
    pe.matmul(out, a[1], b[0], start=False, stop=False)
    return pe.matmul(out, a[0], b[1], start=False, stop=last)


def stand(eng, passed):
    eng.sem_inc(passed, 1)


def linker(eng, order, per_round):
    done = [0]

    def link(ins, i):
        done[0] = done[0] % per_round + 1
        ins.then_inc(order, 1)
        eng.wait_ge(order, i * per_round + done[0])

    return link


def project(nc, x, w_dram, wr_dram, xe, xnt_d, qd, kd, vd, gate_d):
    with ExitStack() as ctx:
        sb, ps, sem = allocators(nc, ctx, "project")
        passed = sem("passed")
        NW = 5
        w = [sb(f"w_{part}", [P, NW, KT, D], F32R) for part in ("hi", "lo")]
        w_raw = [sb(f"w_raw{j}", [P, KT, D]) for j in range(2)]
        wr = sb("wr", [P, KT, E + 1])
        xin = sb("xin", [P, TPB, D])
        xn = sb("xn", [P, TPB, ROW])
        xnT = sb("xnT", [P, KT, BLK])
        xT2 = [sb(f"xT_{part}", [P, KT, BLK], F32R) for part in ("hi", "lo")]
        ident = sb("ident", [P, P])
        before = sb("before", [P, P], BF16)
        ones = sb("ones", [P, P], BF16)
        e_iota = sb("e_iota", [P, E])
        e_slot = sb("e_slot", [P, E])
        iota_i = sb("iota_i", [P, E], I32)
        tok_i = sb("tok_i", [P, TPB], I32)
        tok_f = sb("tok_f", [P, TPB])
        blank = sb("blank", [P, ROW])
        blank_i = sb("blank_i", [P, 1], I32)
        stats = sb("stats", [P, TPB, 6])
        mv = sb("mv", [P, TPB, 2])
        std = sb("std", [P, TPB])
        rstd = sb("rstd", [P, TPB])
        eps = sb("eps", [P, 1])
        lg = sb("lg", [P, TPB, E + 1])
        top = sb("top", [P, TPB, 8])
        topi = sb("topi", [P, TPB, 8], U32)
        ntop = sb("ntop", [P, TPB])
        ex = sb("ex", [P, TPB, TOPK])
        exs = sb("exs", [P, TPB])
        exr = sb("exr", [P, TPB])
        se_e = sb("se_e", [P, TPB])
        gate = sb("gate", [P, NBLK * TPB])
        eq = sb("eq", [P, TPB, TOPK, E])
        mask = sb("mask", [P, TPB, E], BF16)
        carry = sb("carry", [P, E])
        carry_b = sb("carry_b", [P, E], BF16)
        blk_n = sb("blk_n", [P, E])
        over = sb("over", [P, TPB, E])
        slot = sb("slot", [P, TPB, E])
        picked = sb("picked", [P, TPB, TOPK, E])
        idx_f = sb("idx_f", [P, TPB, TOPK])
        idx = sb("idx", [P, TPB, TOPK], U32)
        hi = sb("hi", [P, 2, BLK], F32R)
        lo = sb("lo", [P, 2, BLK], F32R)
        vout = sb("vout", [P, TPB, D])

        p_turn = [ps(f"p_turn{j}", [P, KT, P]) for j in range(2)]
        p_proj = [ps(f"p_proj{j}", [P, BLK]) for j in range(4)]
        p_lg = ps("p_lg", [P, TPB, P])
        p_pos = ps("p_pos", [P, TPB, P])

        w_in = [sem(f"w_in{j}") for j in range(2)]
        w_hi, w_split, x_hi, x_split = map(sem, ("w_hi", "w_split", "x_hi", "x_split"))
        router_in, consts, iotas, blank_ready, blank_out = map(sem, ("router_in", "consts", "iotas", "blank_ready", "blank_out"))
        x_free, x_in, eps_ready, var_ready, std_ready = map(sem, ("x_free", "x_in", "eps_ready", "var_ready", "std_ready"))
        xn_ready, turned, xnT_ready, xnT_out, logits = map(sem, ("xn_ready", "turned", "xnT_ready", "xnT_out", "logits"))
        top_ready, ex_ready, mask_ready, pos_ready, idx_ready = map(sem, ("top_ready", "ex_ready", "mask_ready", "pos_ready", "idx_ready"))
        sent, proj_done, hi_ready, lo_ready, v_ready = map(sem, ("sent", "proj_done", "hi_ready", "lo_ready", "v_ready"))
        out_slot = [sem(f"out_slot{j}") for j in range(2)]
        v_slot = [sem(f"v_slot{j}") for j in range(TPB)]
        norm_order, route_order, gate_ready, gate_out = map(sem, ("norm_order", "route_order", "gate_ready", "gate_out"))

        block = ctx.enter_context(nc.Block())

        @block.sync
        def _(sp):
            for n in range(NW):
                if n >= 2:
                    sp.wait_ge(w_split, (n - 1) * KT)
                sp.dma_start(w_raw[n % 2][:, :, :], w_dram[n].rearrange("(k p) n -> p k n", p=P)).then_inc(w_in[n % 2], 16)
            sp.dma_start(wr[:, :, :], wr_dram.rearrange("(k p) n -> p k n", p=P)).then_inc(router_in, 16)
            with sp.Fori(0, B) as b:
                with sp.Fori(0, BPB) as c:
                    blk = b * BPB + c
                    for n in range(NG):
                        m, ft = n // KT, n % KT
                        for part, stage, ready in ((0, hi, hi_ready), (1, lo, lo_ready)):
                            sp.wait_ge(ready, blk * NG + n + 1)
                            src = stage[:, n % 2, :].bitcast(F32)
                            if m % 2 == 0:
                                dst = qd[bass.ds(b, 1), 4 * ft:4 * ft + 4, bass.ds(c, 1), part * DH:(part + 1) * DH, m // 2, :]
                                dst = dst.rearrange("b h c d t -> (b c h) d t")
                            else:
                                dst = kd[bass.ds(b, 1), 4 * ft:4 * ft + 4, part * DH:(part + 1) * DH, m // 2, bass.ds(c * BLK, BLK)]
                                dst = dst.rearrange("b h d t -> (b h) d t")
                            sp.dma_start(dst, src).then_inc(out_slot[n % 2], 16)
                    for t in range(TPB):
                        sp.wait_ge(v_ready, blk * TPB + t + 1)
                        dst = vd[bass.ds(b, 1), :, :, bass.ds(c * TPB + t, 1), :].rearrange("b h p o d -> p (b o h) d")
                        sp.dma_start(dst, vout[:, t, :].rearrange("p (h d) -> p h d", h=H)).then_inc(v_slot[t], 16)
            sp.wait_ge(gate_ready, NBLK)
            sp.dma_start(gate_d, gate[:, :]).then_inc(gate_out, 16)
            for j in range(2):
                sp.wait_ge(out_slot[j], NBLK * NG // 2 * 32 + 32)
            for t in range(TPB):
                sp.wait_ge(v_slot[t], NBLK * 16 + 16)
            sp.wait_ge(gate_out, 16)

        @block.gpsimd
        def _(pool):
            pool.memset(ident[:, :], 0.0).then_inc(iotas, 1)
            pool.memset(before[:, :], 1.0).then_inc(iotas, 1)
            pool.memset(ones[:, :], 1.0).then_inc(consts, 1)
            pool.memset(blank[:, :], 0.0).then_inc(iotas, 1)
            pool.iota(iota_i[:, :], pattern=[[1, E]], base=0, channel_multiplier=0).then_inc(iotas, 1)
            for a in range(0, P, CAP):
                pool.wait_ge(iotas, 4 + a // CAP)
                pool.wait_ge(consts, 1)
                pool.iota(blank_i[a:a + CAP, :], pattern=[[0, 1]], base=T, channel_multiplier=1).then_inc(iotas, 1)
            pool.wait_ge(iotas, 6)
            pool.iota(tok_i[:, :], pattern=[[P, TPB]], base=0, channel_multiplier=1).then_inc(iotas, 1)
            pool.wait_ge(iotas, 7)
            pool.affine_select(out=ident[:, :], in_=ident[:, :], compare_op=ALU.not_equal, fill=1.0, base=0,
                               pattern=[[-1, P]], channel_multiplier=1).then_inc(consts, 1)
            pool.affine_select(out=before[:, :], in_=before[:, :], compare_op=ALU.is_ge, fill=0.0, base=-1,
                               pattern=[[1, P]], channel_multiplier=-1).then_inc(consts, 1)
            pool.tensor_copy(blank[:, C_TOK:C_TOK + 1], blank_i[:, :]).then_inc(blank_ready, 1)
            pool.tensor_copy(e_iota[:, :], iota_i[:, :]).then_inc(iotas, 1)
            pool.tensor_copy(tok_f[:, :], tok_i[:, :]).then_inc(consts, 1)
            pool.wait_ge(iotas, 8)
            pool.tensor_scalar(e_slot[:, :], e_iota[:, :], float(CAP), None, ALU.mult).then_inc(consts, 1)
            def load(i):
                pool.wait_ge(x_free, i + 1)
                pool.dma_start(xin[:, :, :], x[bass.ds(i * BLK, BLK), :].rearrange("(t p) d -> p t d", p=P)).then_inc(x_in, 16)

            def send(i):
                pool.wait_ge(idx_ready, i + 1)
                stand(pool, passed)
                for t in range(TPB):
                    for k in range(TOPK):
                        pool.indirect_dma_start(xe, bass.IndirectOffsetOnAxis(idx[:, t, k:k + 1], 0), xn[:, t, :], None,
                                                bounds_check=E * CAP - 1, oob_is_err=False).then_inc(sent, 16)

            load(0)
            pool.wait_ge(blank_ready, 1)
            for j in range(E * CAP // P):
                pool.dma_start(xe[j * P:(j + 1) * P, :], blank[:, :]).then_inc(blank_out, 16)
            pool.wait_ge(blank_out, E * CAP // P * 16)
            with pool.Fori(0, NBLK - 1) as i:
                load(i + 1)
                send(i)
            send(NBLK - 1)
            pool.wait_ge(sent, NBLK * TPB * TOPK * 16)

        @block.tensor
        def _(pe):
            pe.wait_ge(consts, 5)
            pe.wait_ge(router_in, 16)
            with pe.Fori(0, NBLK) as i:
                pe.wait_ge(xn_ready, i + 1)
                for t in range(TPB):
                    if t >= 2:
                        pe.wait_ge(xnT_ready, i * TPB + t - 1)
                    for k in range(KT):
                        last = pe.transpose(p_turn[t % 2][:, k, :], xn[:, t, k * P:(k + 1) * P], ident[:, :])
                    last.then_inc(turned, 1)
                pe.wait_ge(x_split, i * TPB + TPB)
                for n in range(NGV):
                    if n % KT == 0:
                        pe.wait_ge(w_split, min(n // KT + 1, NW) * KT)
                    if n >= 4:
                        pe.wait_ge(lo_ready, i * NG + n - 3)
                    for k in range(KT):
                        if n < NG:
                            lhs = [part[:, n // KT, k, (n % KT) * P:(n % KT + 1) * P] for part in w]
                            rhs = [part[:, k, :] for part in xT2]
                        else:
                            lhs = [part[:, k, (n - NG) * P:(n - NG + 1) * P] for part in xT2]
                            rhs = [part[:, 4, k, :] for part in w]
                        last = products(pe, p_proj[n % 4][:, :], lhs, rhs, k == 0, k == KT - 1)
                    last.then_inc(proj_done, 1)
                    if n == 1:
                        for t in range(TPB):
                            for k in range(KT):
                                last = pe.matmul(p_lg[:, t, 0:E + 1], xnT[:, k, t * P:(t + 1) * P], wr[:, k, :],
                                                 start=(k == 0), stop=(k == KT - 1))
                        last.then_inc(logits, 1)
                    if n == 5:
                        pe.wait_ge(mask_ready, i + 1)
                        for t in range(TPB):
                            pe.matmul(p_pos[:, t, 0:E], before[:, :], mask[:, t, :], start=True, stop=False)
                            for t2 in range(t):
                                pe.matmul(p_pos[:, t, 0:E], ones[:, :], mask[:, t2, :], start=False, stop=False)
                            last = pe.matmul(p_pos[:, t, 0:E], ones[:, :], carry_b[:, :], start=False, stop=True)
                        last.then_inc(pos_ready, 1)

        @block.scalar
        def _(act):
            act.sem_inc(out_slot[0], 32)
            act.sem_inc(out_slot[1], 32)
            for t in range(TPB):
                act.sem_inc(v_slot[t], 16)
            act.sem_inc(xnT_out, 64)

            def std_of(i):
                act.wait_ge(var_ready, i + 1)
                act.activation(std[:, :], mv[:, :, 1], ACT.Sqrt, bias=eps[:, 0:1]).then_inc(std_ready, 1)

            def a_block(i, more):
                for t in range(TPB):
                    act.wait_ge(turned, i * TPB + t + 1)
                    if t == 0:
                        act.wait_ge(xnT_out, i * 64 + 64)
                    act.activation(xT2[0][:, :, t * P:(t + 1) * P], p_turn[t % 2][:, :, :], ACT.Copy).then_inc(x_hi, 1)
                    act.activation(xnT[:, :, t * P:(t + 1) * P], p_turn[t % 2][:, :, :], ACT.Copy).then_inc(xnT_ready, 1)
                act.wait_ge(x_split, i * TPB + TPB)
                stand(act, passed)
                for part in range(2):
                    for half in range(BLK // SBLK):
                        act.dma_start(xnt_d[bass.ds(i * (BLK // SBLK) + half, 1), :, part, :, :].rearrange("o p k t -> (o p) k t"),
                                      xT2[part][:, :, half * SBLK:(half + 1) * SBLK].bitcast(F32)).then_inc(xnT_out, 16)
                for n in range(NGV):
                    if n == 2:
                        act.wait_ge(top_ready, i + 1)
                        for t in range(TPB):
                            act.activation(ex[:, t, :], top[:, t, 0:TOPK], ACT.Exp, bias=ntop[:, t:t + 1],
                                           accum_out=exs[:, t:t + 1]).then_inc(ex_ready, 1)
                        act.activation(se_e[:, :], lg[:, :, E], ACT.Exp, scale=-1.0).then_inc(ex_ready, 1)
                    act.wait_ge(proj_done, i * NGV + n + 1)
                    if n < NG:
                        act.wait_ge(out_slot[n % 2], (i * (NG // 2) + n // 2) * 32 + 32)
                        act.activation(hi[:, n % 2, :], p_proj[n % 4][:, :], ACT.Copy,
                                       scale=Q_SCALE if (n // KT) % 2 == 0 else 1.0).then_inc(hi_ready, 1)
                    else:
                        v = n - NG
                        act.wait_ge(v_slot[v], i * 16 + 16)
                        act.activation(vout[:, v, :], p_proj[n % 4][:, :], ACT.Copy).then_inc(v_ready, 1)
                    if more and n == 11:
                        std_of(i + 1)

            act.wait_ge(eps_ready, 2)
            std_of(0)
            for n in range(NW):
                act.wait_ge(w_in[n % 2], n // 2 * 16 + 16)
                for k in range(KT):
                    act.activation(w[0][:, n, k, :], w_raw[n % 2][:, k, :], ACT.Copy).then_inc(w_hi, 1)
            with act.Fori(0, NBLK - 1) as i:
                a_block(i, True)
            a_block(NBLK - 1, False)
            act.wait_ge(xnT_out, NBLK * 64 + 64)

        @block.vector
        def _(dve):
            dve.memset(eps[:, :], LN_EPS).then_inc(eps_ready, 1)
            dve.memset(carry[:, :], 0.0).then_inc(eps_ready, 1)
            dve.memset(xn[:, :, D:ROW], 0.0).then_inc(eps_ready, 1)
            dve.memset(carry_b[:, :], 0.0).then_inc(x_free, 1)
            dve.wait_ge(consts, 5)
            nlink = linker(dve, norm_order, TPB + 1)
            rlink = linker(dve, route_order, 17)

            def norm_stats(i):
                dve.wait_ge(x_in, i * 16 + 16)
                for t in range(TPB):
                    nlink(dve.bn_stats(stats[:, t, :], xin[:, t, :]), i)
                stand(dve, passed)
                for t in range(TPB):
                    last = dve.bn_aggr(mv[:, t, :], stats[:, t, :])
                last.then_inc(var_ready, 1)

            def norm_rows(i):
                dve.wait_ge(std_ready, i + 1)
                nlink(dve.reciprocal(rstd[:, :], std[:, :]), i)
                dve.wait_ge(var_ready, i + 1)
                if not isinstance(i, int) or i:
                    dve.wait_ge(sent, i * (TPB * TOPK * 16))
                for t in range(TPB):
                    last = dve.tensor_scalar(xn[:, t, 0:D], xin[:, t, :], mv[:, t, 0:1], rstd[:, t:t + 1], ALU.subtract, ALU.mult)
                last.then_inc(xn_ready, 1)
                dve.tensor_copy(xn[:, :, C_TOK], tok_f[:, :]).then_inc(x_free, 1)

            def split_x(i):
                for t in range(TPB):
                    dve.wait_ge(xnT_ready, i * TPB + t + 1)
                    dve.wait_ge(x_hi, i * TPB + t + 1)
                    xt = slice(t * P, (t + 1) * P)
                    dve.tensor_tensor(xT2[1][:, :, xt], xnT[:, :, xt], xT2[0][:, :, xt].bitcast(F32), ALU.subtract).then_inc(x_split, 1)

            def route(i):
                dve.wait_ge(logits, i + 1)
                rlink(dve.tensor_copy(lg[:, :, :], p_lg[:, :, 0:E + 1]), i)
                stand(dve, passed)
                for t in range(TPB):
                    last = dve.max(top[:, t, :], lg[:, t, 0:E])
                rlink(last, i)
                stand(dve, passed)
                for t in range(TPB):
                    last = dve.max_index(topi[:, t, :], top[:, t, :], lg[:, t, 0:E])
                rlink(last, i)
                dve.tensor_scalar(ntop[:, :], top[:, :, 0], -1.0, None, ALU.mult).then_inc(top_ready, 1)
                rlink(dve.tensor_copy(xn[:, :, C_E:C_E + TOPK], topi[:, :, 0:TOPK]), i)
                rlink(dve.tensor_tensor(eq[:, :, :, :],
                                        e_iota[:, :].rearrange("p (a b e) -> p a b e", a=1, b=1).broadcast_to([P, TPB, TOPK, E]),
                                        xn[:, :, C_E:C_E + TOPK].rearrange("p t (k a) -> p t k a", a=1).broadcast_to([P, TPB, TOPK, E]),
                                        ALU.is_equal), i)
                with nc.allow_low_precision(reason="0 or 1"):
                    rlink(dve.tensor_reduce(mask[:, :, :], eq[:, :, :, :].rearrange("p t k e -> p t e k"), AX_X, ALU.add), i)
                dve.tensor_reduce(blk_n[:, :], mask[:, :, :].rearrange("p t e -> p e t"), AX_X, ALU.add).then_inc(mask_ready, 1)
                dve.wait_ge(ex_ready, i * (TPB + 1) + TPB + 1)
                rlink(dve.reciprocal(exr[:, :], exs[:, :]), i)
                rlink(dve.tensor_tensor(xn[:, :, C_W:C_W + TOPK], ex[:, :, :],
                                        exr[:, :].rearrange("p (t a) -> p t a", a=1).broadcast_to([P, TPB, TOPK]), ALU.mult), i)
                rlink(dve.tensor_scalar(se_e[:, :], se_e[:, :], 1.0, None, ALU.add), i)
                dve.reciprocal(gate[:, bass.ds(i * TPB, TPB)], se_e[:, :]).then_inc(gate_ready, 1)

            def place(i):
                dve.wait_ge(pos_ready, i + 1)
                rlink(dve.tensor_scalar(over[:, :, :], p_pos[:, :, 0:E], CAP - 0.5, FAR, ALU.is_gt, ALU.mult), i)
                rlink(dve.tensor_tensor(slot[:, :, :], p_pos[:, :, 0:E],
                                        e_slot[:, :].rearrange("p (a e) -> p a e", a=1).broadcast_to([P, TPB, E]), ALU.add), i)
                dve.wait_ge(mask_ready, i + 1)
                rlink(dve.tensor_tensor(carry[:, :], carry[:, :], blk_n[:, :], ALU.add), i)
                rlink(dve.tensor_tensor(slot[:, :, :], slot[:, :, :], over[:, :, :], ALU.add), i)
                rlink(dve.tensor_tensor(picked[:, :, :, :], eq[:, :, :, :],
                                        slot[:, :, :].rearrange("p t (a e) -> p t a e", a=1).broadcast_to([P, TPB, TOPK, E]),
                                        ALU.mult), i)
                rlink(dve.tensor_reduce(idx_f[:, :, :], picked[:, :, :, :], AX_X, ALU.add), i)
                rlink(dve.tensor_copy(carry_b[:, :], carry[:, :]), i)
                dve.tensor_copy(idx[:, :, :], idx_f[:, :, :]).then_inc(idx_ready, 1)
                rlink(dve.tensor_scalar(tok_f[:, :], tok_f[:, :], float(BLK), None, ALU.add), i)

            def split(i, ns):
                for n in ns:
                    dve.wait_ge(hi_ready, i * NG + n + 1)
                    dve.scalar_tensor_tensor(lo[:, n % 2, :], p_proj[n % 4][:, :], Q_SCALE if (n // KT) % 2 == 0 else 1.0,
                                             hi[:, n % 2, :].bitcast(F32), ALU.mult, ALU.subtract).then_inc(lo_ready, 1)

            def v_block(i, more):
                split_x(i)
                split(i, range(0, 2))
                route(i)
                split(i, range(2, 6))
                place(i)
                split(i, range(6, 8))
                if more:
                    norm_stats(i + 1)
                split(i, range(8, 14))
                if more:
                    norm_rows(i + 1)
                split(i, range(14, NG))

            norm_stats(0)
            norm_rows(0)
            for n in range(NW):
                for k in range(KT):
                    dve.wait_ge(w_hi, n * KT + k + 1)
                    dve.tensor_tensor(w[1][:, n, k, :], w_raw[n % 2][:, k, :], w[0][:, n, k, :].bitcast(F32), ALU.subtract)\
                       .then_inc(w_split, 1)
            with dve.Fori(0, NBLK - 1) as i:
                v_block(i, True)
            v_block(NBLK - 1, False)
            dve.wait_ge(idx_ready, NBLK)


HALF = S // 2
TILES = ITERS * TPB
PAIRS = TILES // 2
HUGE = 3.0e38
TURN, MEET, MET, LEAVE = 3, 5, 6, 7
DVE_READS = [(t, 0) for t in (0, 2, 3)]
DVE_JOINS = [0, 1, 3]
ACT_READS = [(t, n) for t in range(TPB) for n in range(4) if (t, n) not in DVE_READS]


def tile_of(i, t, back):
    d, place = divmod(t - back, TPB)
    if isinstance(i, int) and not 0 <= i + d < ITERS:
        return None
    return i + d, place


def attend(nc, qd, kd, vd, lam, od):
    with ExitStack() as ctx:
        sb, ps, sem = allocators(nc, ctx, "attend")
        passed = sem("passed")
        q = [sb(f"q{t}", [P, 2, P], F32R) for t in range(TPB)]
        k = sb("k", [P, 2, 2, S], F32R)
        v = sb("v", [P, S // P, DH])
        p = [[sb(f"p{m + 1}_{t}", [P, S]) for m in range(2)] for t in range(TPB)]
        aT = [sb(f"aT{t}", [P, S // P, 2 * P]) for t in range(2)]
        ident = sb("ident", [P, P])
        fold = sb("fold", [P, DH])
        lamb = sb("lamb", [P, H])
        low = sb("low", [P, TPB, 2])
        nmax = sb("nmax", [P, TPB, 2])
        sums = sb("sums", [P, TPB, 2])
        recip = sb("recip", [P, TPB, 2])
        coef1 = sb("coef1", [P, 1])
        coef = sb("coef", [P, 1])
        keep = sb("keep", [P, 2, 2])
        o_sb = sb("o_sb", [P, 2 * P])
        o_out = [sb(f"o_out{j}", [P, 2, DH]) for j in range(2)]
        p_s = [ps(f"p_s{j}", [P, HALF]) for j in range(2)]
        p_t = [ps(f"p_t{j}", [P, TPB, P]) for j in range(2)]
        p_o = ps("p_o", [P, 2 * P])
        p_f = ps("p_f", [P, 2, DH])

        lam_in, consts, iotas, k_in, v_in = map(sem, ("lam_in", "consts", "iotas", "k_in", "v_in"))
        q_in = [sem(f"q_in{t}") for t in range(TPB)]
        scores, lifted, expd, recipd, coefs, scaled = map(sem, ("scores", "lifted", "expd", "recipd", "coefs", "scaled"))
        joined = sem("joined")
        turned, read_dve, read_act, av_done, o_read, folded, o_ready, kept = map(
            sem, ("turned", "read_dve", "read_act", "av_done", "o_read", "folded", "o_ready", "kept"))
        o_slot = [sem(f"o_slot{j}") for j in range(2)]
        block = ctx.enter_context(nc.Block())

        def reads(i, t, n):
            if (t, n) in DVE_READS:
                return read_dve, i * len(DVE_READS) + DVE_READS.index((t, n)) + 1
            return read_act, i * len(ACT_READS) + ACT_READS.index((t, n)) + 1

        def run(eng, step):
            for i in range(2):
                for t in range(TPB):
                    step(i, t)
            with eng.Fori(2, ITERS) as i:
                for t in range(TPB):
                    step(i, t)
            for n in range(LEAVE - 1):
                step(ITERS + n // TPB, n % TPB)

        @block.sync
        def _(sp):
            def loads(i, new_head=None, v_head=None):
                for t in range(TPB):
                    if not isinstance(i, int) or i:
                        sp.wait_ge(scores, i * 16 - 16 + 4 * t + 4)
                    if t == 0 and new_head is not None:
                        for part in range(2):
                            for dup in range(2):
                                r = part * 64 + dup * DH
                                sp.dma_start(k[r:r + DH, bass.ds(new_head % 2, 1), :, :].bitcast(F32).rearrange("p o m t -> p (o m) t"),
                                             kd[bass.ds(new_head, 1), part * DH:(part + 1) * DH, :, :].rearrange("o p m t -> (o p) m t"))\
                                  .then_inc(k_in, 16)
                    for dup in range(2):
                        sp.dma_start(q[t][dup * 64:dup * 64 + 64, :, :].bitcast(F32),
                                     qd[bass.ds(i, 1), :, :, t * P:(t + 1) * P].rearrange("o p m t -> (o p) m t")).then_inc(q_in[t], 16)
                    if t == 3 and v_head is not None:
                        if not isinstance(v_head, int) or v_head:
                            sp.wait_ge(av_done, v_head * (S // P // 2))
                        sp.dma_start(v[:, :, :], vd[bass.ds(v_head, 1), :, :, :].rearrange("o p t d -> (o p) t d")).then_inc(v_in, 16)
                    if t % 2:
                        done = tile_of(i, t, TPB + LEAVE)
                        if done:
                            results(done[0], done[1] // 2)

            def results(i, j):
                sp.wait_ge(o_ready, i * 2 + j + 1)
                stand(sp, passed)
                dst = od[bass.ds(i // (H * BPB), 1), bass.ds(i % BPB, 1), 2 * j:2 * j + 2, :, bass.ds((i // BPB) % H, 1), :]
                sp.dma_start(dst.rearrange("b c t p h d -> (b c h p) t d"), o_out[j][:, :, :])\
                  .then_inc(o_slot[j], 16)

            sp.dma_start(lamb[:, :], lam.broadcast_to([P, H])).then_inc(lam_in, 16)
            loads(0, new_head=0, v_head=0)
            for i in range(1, BPB):
                loads(i)
            with sp.Fori(1, HEADS) as g:
                loads(g * BPB, new_head=g)
                loads(g * BPB + 1, v_head=g)
                with sp.Fori(2, BPB) as c:
                    loads(g * BPB + c)
            for n in range(PAIRS - 5, PAIRS):
                results(n // 2, n % 2)
            for j in range(2):
                sp.wait_ge(o_slot[j], ITERS * 16 + 16)

        @block.tensor
        def _(pe):
            def half(i, t, n):
                if n == 0:
                    pe.wait_ge(q_in[t], i * 32 + 32)
                    if t == 0:
                        pe.wait_ge(k_in, (i // BPB) * 64 + 64)
                if not isinstance(i, int) or i or t or n >= 2:
                    pe.wait_ge(lifted, i * 16 + 4 * t + n - 1)
                for c in range(2):
                    at = (n % 2) * HALF + c * 512
                    last = pe.matmul(p_s[n % 2][:, c * 512:(c + 1) * 512], q[t][:, n // 2, :],
                                     k[:, bass.ds((i // BPB) % 2, 1), n // 2, at:at + 512].rearrange("p o t -> p (o t)"),
                                     start=True, stop=True)
                last.then_inc(scores, 1)

            def turn(i, t, n):
                added = n == 1 or n == 0 and t in DVE_JOINS
                if n == 0 and added:
                    pe.wait_ge(joined, i * len(DVE_JOINS) + DVE_JOINS.index(t) + 1)
                elif n == 0:
                    pe.wait_ge(scaled, (i * 4 + t) * 2 + 1)
                elif n < 3:
                    pe.wait_ge(scaled, (i * 4 + t) * 2 + n)
                if n >= 2:
                    pe.wait_ge(*reads(i, t, n - 2))
                elif not isinstance(i, int) or i or t:
                    pe.wait_ge(*reads(*((i, t - 1) if t else (i - 1, TPB - 1)), n + 2))
                for c in range(4):
                    at = (4 * n + c) * P
                    last = pe.matmul(p_t[n % 2][:, c, :], p[t][0][:, at:at + P], ident[:, :], start=True, stop=added,
                                     is_transpose=True)
                    if not added:
                        last = pe.matmul(p_t[n % 2][:, c, :], p[t][1][:, at:at + P], ident[:, :], start=False, stop=True,
                                         is_transpose=True)
                last.then_inc(turned, 1)

            def meet(i, j, n):
                if n == 0:
                    pe.wait_ge(o_read, i * 2 + j + 1)
                    pe.wait_ge(v_in, (i // BPB) * 16 + 16)
                    pe.wait_ge(*reads(i, 2 * j + 1, 3))
                    pe.wait_ge(*reads(i, 2 * j, 0))
                for c in range(4):
                    last = pe.matmul(p_o[c * DH:(c + 1) * DH, :], v[:, 4 * n + c, :], aT[j][:, 4 * n + c, :],
                                     start=(n == 0), stop=(n == 3), tile_position=(0, c * DH))
                if n == 3:
                    last.then_inc(av_done, 1)

            def fold_o(i, j):
                pe.wait_ge(o_read, i * 2 + j + 2)
                if not isinstance(i, int) or i or j:
                    pe.wait_ge(o_ready, i * 2 + j)
                for c in range(2):
                    last = pe.matmul(p_f[:, c, :], o_sb[:, c * P:(c + 1) * P], fold[:, :], start=True, stop=True)
                last.then_inc(folded, 1)

            def step(i, t):
                here, old, meets, met, left = (tile_of(i, t, b) for b in (0, TURN, MEET, MET, LEAVE))
                if here:
                    half(i, t, 0)
                if t % 2 == 0 and met:
                    meet(met[0], met[1] // 2, 2)
                if old:
                    turn(*old, 0)
                if here:
                    half(i, t, 1)
                if old:
                    turn(*old, 1)
                if here:
                    half(i, t, 2)
                if t % 2 and meets:
                    meet(meets[0], meets[1] // 2, 0)
                    meet(meets[0], meets[1] // 2, 1)
                if t % 2 == 0 and met:
                    meet(met[0], met[1] // 2, 3)
                if old:
                    turn(*old, 2)
                if t % 2 and left:
                    fold_o(left[0], left[1] // 2)
                if here:
                    half(i, t, 3)
                if old:
                    turn(*old, 3)

            pe.wait_ge(consts, 2)
            run(pe, step)

        @block.scalar
        def _(act):
            def read(i, t, n):
                act.wait_ge(turned, (i * 4 + t) * 4 + n + 1)
                act.activation(aT[t // 2][:, 4 * n:4 * n + 4, (t % 2) * P:(t % 2 + 1) * P], p_t[n % 2][:, :, :], ACT.Copy)\
                   .then_inc(read_act, 1)

            def exp(i, t, m):
                act.wait_ge(lifted, (i * 4 + t) * 4 + 2 * m + 2)
                act.activation(p[t][m][:, :], p[t][m][:, :], ACT.Exp, bias=nmax[:, t, m:m + 1], scale=-1.0,
                               accum_out=sums[:, t, m:m + 1]).then_inc(expd, 1)

            def step(i, t):
                here, last, old, met = (tile_of(i, t, b) for b in (0, 1, TURN, MET))
                if last:
                    exp(*last, 1)
                if old:
                    if (old[1], 0) in ACT_READS:
                        read(*old, 0)
                    read(*old, 1)
                if here:
                    exp(i, t, 0)
                if old:
                    read(*old, 2)
                    read(*old, 3)
                if t % 2 == 0 and met:
                    act.wait_ge(av_done, met[0] * 2 + met[1] // 2 + 1)
                    act.activation(o_sb[:, :], p_o[:, :], ACT.Copy).then_inc(o_read, 1)

            act.sem_inc(o_read, 1)
            run(act, step)

        @block.vector
        def _(dve):
            def lift(i, t, n):
                m = n // 2
                dve.wait_ge(scores, i * 16 + 4 * t + n + 1)
                if n == 0 and (not isinstance(i, int) or i):
                    dve.wait_ge(turned, (i * 4 + t) * 4 - 12)
                if n % 2:
                    dve.wait_ge(lifted, i * 16 + 4 * t + n)
                at = (n % 2) * HALF
                dve.tensor_scalar(p[t][m][:, at:at + HALF], p_s[n % 2][:, :], -1.0, low[:, t, m:m + 1] if n % 2 else HUGE,
                                  ALU.mult, ALU.min, accum_out=(nmax if n % 2 else low)[:, t, m:m + 1]).then_inc(lifted, 1)

            def step(i, t):
                here, last, old, met, left = (tile_of(i, t, b) for b in (0, 1, TURN, MEET, LEAVE))
                if here:
                    lift(i, t, 0)
                if old and (old[1], 0) in DVE_READS:
                    dve.wait_ge(turned, (old[0] * 4 + old[1]) * 4 + 1)
                    ot = old[1]
                    dve.tensor_copy(aT[ot // 2][:, 0:4, (ot % 2) * P:(ot % 2 + 1) * P], p_t[0][:, :, :]).then_inc(read_dve, 1)
                if here:
                    lift(i, t, 1)
                if t % 2 and met:
                    j = met[1] // 2
                    if not here:
                        dve.wait_ge(o_ready, met[0] * 2 + j - 1)
                    dve.wait_ge(recipd, met[0] * 4 + 2 * j + 2)
                    dve.tensor_copy(keep[:, j, :], recip[:, 2 * j:2 * j + 2, 0]).then_inc(kept, 1)
                if last:
                    if t % 2 and met:
                        dve.wait_ge(kept, met[0] * 2 + met[1] // 2 + 1)
                    dve.wait_ge(expd, (last[0] * 4 + last[1]) * 2 + 2)
                    dve.reciprocal(recip[:, last[1], :], sums[:, last[1], :]).then_inc(recipd, 1)
                if here:
                    lift(i, t, 2)
                if last and last[1] in DVE_JOINS:
                    dve.wait_ge(coefs, (last[0] * 4 + last[1]) * 3 + 2)
                    p1, p2 = (p[last[1]][m][:, 0:S // 4] for m in range(2))
                    dve.scalar_tensor_tensor(p1, p2, coef[:, 0:1], p1, ALU.mult, ALU.add).then_inc(joined, 1)
                if t % 2 and left:
                    j = left[1] // 2
                    dve.wait_ge(folded, left[0] * 2 + j + 1)
                    dve.wait_ge(kept, left[0] * 2 + j + 1)
                    dve.wait_ge(o_slot[j], left[0] * 16 + 16)
                    dve.tensor_tensor(o_out[j][:, :, :], p_f[:, :, :],
                                      keep[:, j, :].rearrange("p (c a) -> p c a", a=1).broadcast_to([P, 2, DH]), ALU.mult)\
                       .then_inc(o_ready, 1)
                if here:
                    lift(i, t, 3)

            for j in range(2):
                dve.sem_inc(o_slot[j], 16)
            run(dve, step)

        @block.gpsimd
        def _(pool):
            pool.memset(ident[:, :], 0.0).then_inc(iotas, 1)
            pool.memset(fold[:, :], 0.0).then_inc(iotas, 1)
            pool.wait_ge(iotas, 2)
            pool.affine_select(out=ident[:, :], in_=ident[:, :], compare_op=ALU.not_equal, fill=1.0, base=0,
                               pattern=[[-1, P]], channel_multiplier=1).then_inc(consts, 1)
            for a in range(4):
                pool.affine_select(out=fold[:, :], in_=fold[:, :], compare_op=ALU.not_equal, fill=1.0, base=-a * DH,
                                   pattern=[[-1, DH]], channel_multiplier=1).then_inc(consts if a == 3 else iotas, 1)
                if a < 3:
                    pool.wait_ge(iotas, 3 + a)
            pool.wait_ge(lam_in, 16)
            pool.tensor_scalar(lamb[:, :], lamb[:, :], -1.0, None, ALU.mult).then_inc(iotas, 1)
            pool.wait_ge(iotas, 6)

            def scale(i, h, t):
                n = i * 4 + t
                pool.wait_ge(expd, 2 * n + 2)
                stand(pool, passed)
                pool.tensor_tensor(coef1[:, :], sums[:, t, 0:1], lamb[:, bass.ds(h, 1)], ALU.mult).then_inc(coefs, 1)
                pool.wait_ge(coefs, 3 * n + 1)
                pool.wait_ge(recipd, n + 1)
                pool.tensor_tensor(coef[:, :], coef1[:, :], recip[:, t, 1:2], ALU.mult).then_inc(coefs, 1)
                pool.wait_ge(coefs, 3 * n + 2)
                g1, g23 = slice(S // 4, HALF), slice(HALF, S)
                g = slice(S // 4 if t in DVE_JOINS else 0, HALF)
                pool.tensor_tensor(p[t][1][:, g], p[t][1][:, g], coef[:, 0:1].broadcast_to([P, g.stop - g.start]), ALU.mult).then_inc(coefs, 1)
                pool.wait_ge(coefs, 3 * n + 3)
                pool.tensor_tensor(p[t][0][:, g1], p[t][0][:, g1], p[t][1][:, g1], ALU.add).then_inc(scaled, 1)
                pool.tensor_tensor(p[t][1][:, g23], p[t][1][:, g23], coef[:, 0:1].broadcast_to([P, HALF]), ALU.mult).then_inc(scaled, 1)

            with pool.Fori(0, B) as b:
                with pool.Fori(0, H) as h:
                    with pool.Fori(0, BPB) as c:
                        for t in range(TPB):
                            scale((b * H + h) * BPB + c, h, t)


def shared(nc, xnt_d, gate_d, wsg, wsu, wsd, acc):
    with ExitStack() as ctx:
        sb, ps, sem = allocators(nc, ctx, "shared")
        wg, wu = ([sb(f"{name}_{part}", [P, KT, FS], F32R) for part in ("hi", "lo")] for name in ("wg", "wu"))
        wd = [sb(f"wd_{part}", [P, FSN, D], F32R) for part in ("hi", "lo")]
        raw = [sb(f"raw{j}", [P, 2, KT, P]) for j in range(2)]
        raw_d = [sb(f"raw_d{j}", [P, D]) for j in range(2)]
        gate = sb("gate3", [P, NBLK * TPB])
        gcol = sb("gcol", [P, TPS])
        xT = sb("sxT", [P, 2, KT, SBLK], F32R)
        th = sb("th", [P, 2, SBLK])
        gg = sb("gg", [P, 2, SBLK])
        h = sb("h", [P, 2, SBLK])
        hT = [sb(f"hT_{part}", [P, FSN, SBLK], F32R) for part in ("hi", "lo")]
        y = sb("y", [P, 2, D])
        zero = sb("zero", [CAP, D])
        p_g = [ps(f"p_g{j}", [P, BLK]) for j in range(2)]
        p_u = [ps(f"p_u{j}", [P, BLK]) for j in range(2)]
        p_y = [ps(f"p_y{j}", [P, D]) for j in range(2)]
        gu_in = [sem(f"sgu_in{j}") for j in range(2)]
        wd_in = [sem(f"swd_in{j}") for j in range(2)]
        gate_in, x_in, zeroed, zero_out = map(sem, ("gate_in", "xT_in", "zeroed", "zero_out"))
        w_hi, w_split, d_hi, d_split, hi_ready = map(sem, ("sw_hi", "sw_split", "sd_hi", "sd_split", "sh_hi"))
        g_done, u_done, th_ready, gg_ready, f_ready, h_ready, y_done, gcol_ready, y_ready = map(
            sem, ("g_done", "u_done", "th_ready", "gg_ready", "f_ready", "h_ready", "y_done", "gcol_ready", "y_ready"))
        y_slot = [sem(f"y_slot{j}") for j in range(2)]
        block = ctx.enter_context(nc.Block())

        def gu_piece(f, n):
            return [part[:, :, f * P:(f + 1) * P] for part in (wg, wu)[n]]

        @block.sync
        def _(sp):
            def load(i):
                sp.dma_start(xT[:, :, :, :].bitcast(F32).rearrange("p s k t -> p (s k t)"),
                             xnt_d[bass.ds(i, 1), :, :, :, :].rearrange("o p s k t -> (o p) (s k t)")).then_inc(x_in, 16)

            def load_d(f):
                if f >= 2:
                    sp.wait_ge(d_split, f - 1)
                sp.dma_start(raw_d[f % 2][:, :], wsd[f * P:(f + 1) * P, :]).then_inc(wd_in[f % 2], 16)

            def store(i):
                for t in range(TPS):
                    sp.wait_ge(y_ready, i * TPS + t + 3)
                    sp.dma_start(acc[bass.ds(i * SBLK + t * P, P), :], y[:, t, :]).then_inc(y_slot[t], 16)

            for f in range(FSN):
                if f >= 2:
                    sp.wait_ge(w_split, 2 * f - 2)
                for n, dram in enumerate((wsg, wsu)):
                    sp.dma_start(raw[f % 2][:, n, :, :], dram[:, f * P:(f + 1) * P].rearrange("(k p) n -> p k n", p=P)).then_inc(gu_in[f % 2], 16)
                if f == 0:
                    load(0)
                    sp.dma_start(gate[:, :], gate_d).then_inc(gate_in, 16)
                if f >= 2:
                    load_d(f - 2)
            load_d(FSN - 2)
            load_d(FSN - 1)
            sp.wait_ge(zeroed, 1)
            sp.dma_start(acc[T:T + CAP, :], zero[:, :]).then_inc(zero_out, 16)
            with sp.Fori(1, NSB) as i:
                sp.wait_ge(u_done, i * FSN)
                load(i)
                store(i - 1)
            store(NSB - 1)
            sp.wait_ge(zero_out, 16)
            for j in range(2):
                sp.wait_ge(y_slot[j], NSB * 16 + 16)

        @block.gpsimd
        def _(pool):
            pool.memset(zero[:, :], 0.0).then_inc(zeroed, 1)

        @block.tensor
        def _(pe):
            def one(i, first=False):
                pe.wait_ge(x_in, i * 16 + 16)
                for f in range(FSN):
                    if f >= 2:
                        pe.wait_ge(f_ready, i * FSN + f - 1)
                    for n, (w, p, done) in enumerate(((wg, p_g, g_done), (wu, p_u, u_done))):
                        if first:
                            pe.wait_ge(w_split, 2 * f + n + 1)
                        for k in range(KT):
                            last = products(pe, p[f % 2][:, 0:SBLK], [part[:, k, f * P:(f + 1) * P] for part in w],
                                            [xT[:, part, k, :] for part in range(2)], k == 0, k == KT - 1)
                        last.then_inc(done, 1)
                for t in range(TPS):
                    pe.wait_ge(y_ready, i * TPS + t + 1)
                    for f in range(FSN):
                        if t == 0:
                            pe.wait_ge(h_ready, i * FSN + f + 1)
                            if first:
                                pe.wait_ge(d_split, f + 1)
                        last = products(pe, p_y[t][:, :], [part[:, f, t * P:(t + 1) * P] for part in hT],
                                        [part[:, f, :] for part in wd], f == 0, f == FSN - 1)
                    last.then_inc(y_done, 1)

            one(0, first=True)
            with pe.Fori(1, NSB) as i:
                one(i)

        @block.scalar
        def _(act):
            act.sem_inc(y_ready, 2)
            act.sem_inc(y_slot[0], 16)
            act.sem_inc(y_slot[1], 16)
            def halve_gu(f):
                act.wait_ge(gu_in[f % 2], f // 2 * 32 + 32)
                for n in range(2):
                    act.activation(gu_piece(f, n)[0], raw[f % 2][:, n, :, :], ACT.Copy).then_inc(w_hi, 1)

            def halve_d(f):
                act.wait_ge(wd_in[f % 2], f // 2 * 16 + 16)
                act.activation(wd[0][:, f, :], raw_d[f % 2][:, :], ACT.Copy).then_inc(d_hi, 1)

            def one(i, first=False):
                for f in range(FSN + 1):
                    if f < FSN:
                        if first and f < FSN - 2:
                            halve_gu(f + 2)
                        act.wait_ge(g_done, i * FSN + f + 1)
                        act.activation(th[:, f % 2, :], p_g[f % 2][:, 0:SBLK], ACT.Tanh, scale=0.5).then_inc(th_ready, 1)
                    if first and f:
                        halve_d(f - 1)
                    if f:
                        act.wait_ge(f_ready, i * FSN + f)
                        act.activation(hT[0][:, f - 1, :], h[:, (f - 1) % 2, :], ACT.Copy).then_inc(hi_ready, 1)
                act.wait_ge(gcol_ready, i + 1)
                for t in range(TPS):
                    act.wait_ge(y_done, i * TPS + t + 1)
                    act.wait_ge(y_slot[t], i * 16 + 16)
                    act.activation(y[:, t, :], p_y[t][:, :], ACT.Copy, scale=gcol[:, t:t + 1]).then_inc(y_ready, 1)

            for f in range(2):
                halve_gu(f)
            one(0, first=True)
            with act.Fori(1, NSB) as i:
                one(i)

        @block.vector
        def _(dve):
            def rest_gu(f):
                for n in range(2):
                    w_h, w_l = gu_piece(f, n)
                    dve.wait_ge(w_hi, 2 * f + n + 1)
                    dve.tensor_tensor(w_l, raw[f % 2][:, n, :, :], w_h.bitcast(F32), ALU.subtract).then_inc(w_split, 1)

            def rest_d(f):
                dve.wait_ge(d_hi, f + 1)
                dve.tensor_tensor(wd[1][:, f, :], raw_d[f % 2][:, :], wd[0][:, f, :].bitcast(F32), ALU.subtract).then_inc(d_split, 1)

            def one(i, first=False):
                for f in range(FSN + 1):
                    if f < FSN:
                        if first and f < FSN - 2:
                            rest_gu(f + 2)
                        dve.wait_ge(th_ready, i * FSN + f + 1)
                        dve.scalar_tensor_tensor(gg[:, f % 2, :], th[:, f % 2, :], 1.0, p_g[f % 2][:, 0:SBLK], ALU.add, ALU.mult)\
                           .then_inc(gg_ready, 1)
                        dve.wait_ge(gg_ready, i * FSN + f + 1)
                        dve.wait_ge(u_done, i * FSN + f + 1)
                        dve.scalar_tensor_tensor(h[:, f % 2, :], gg[:, f % 2, :], 0.5, p_u[f % 2][:, 0:SBLK], ALU.mult, ALU.mult)\
                           .then_inc(f_ready, 1)
                    if first and f:
                        rest_d(f - 1)
                    if f:
                        dve.wait_ge(hi_ready, i * FSN + f)
                        dve.tensor_tensor(hT[1][:, f - 1, :], h[:, (f - 1) % 2, :], hT[0][:, f - 1, :].bitcast(F32), ALU.subtract)\
                           .then_inc(h_ready, 1)
                dve.wait_ge(y_ready, i * TPS + 2)
                dve.tensor_copy(gcol[:, :], gate[:, bass.ds(i * TPS, TPS)]).then_inc(gcol_ready, 1)

            for f in range(2):
                rest_gu(f)
            dve.wait_ge(gate_in, 16)
            one(0, first=True)
            with dve.Fori(1, NSB) as i:
                one(i)


def experts(nc, xe, wge, wue, wde, acc):
    with ExitStack() as ctx:
        sb, ps, sem = allocators(nc, ctx, "experts")
        passed = sem("passed")
        wg = [sb(f"ewg{j}", [P, KT, F]) for j in range(ESLOTS)]
        wu = [sb(f"ewu{j}", [P, KT, F]) for j in range(ESLOTS)]
        wd = [sb(f"ewd{j}", [P, FN, D]) for j in range(ESLOTS)]
        rows = [sb(f"rows{j}", [CAP, ROW]) for j in range(ESLOTS)]
        xT = sb("exT", [P, KT, CAP])
        th = sb("eth", [P, FN, CAP])
        gg = sb("egg", [P, FN, CAP])
        hT = [sb(f"ehT{j}", [P, FN, CAP]) for j in range(2)]
        ye = [sb(f"ye{j}", [CAP, D]) for j in range(2)]
        tok = [sb(f"tok{j}", [CAP, 1], U32) for j in range(2)]
        mine = sb("mine", [CAP, TOPK])
        weight = [sb(f"weight{j}", [CAP, 1]) for j in range(2)]
        now = sb("now", [CAP, 1])
        ident = sb("ident4", [P, P])
        p_x = ps("p_x", [P, KT, P])
        p_g = ps("ep_g", [P, FN, CAP])
        p_u = ps("ep_u", [P, FN, CAP])
        p_y = [ps(f"ep_y{j}", [CAP, D]) for j in range(2)]
        rows_in = [sem(f"rows_in{j}") for j in range(ESLOTS)]
        gu_in = [sem(f"gu_in{j}") for j in range(ESLOTS)]
        wd_in = [sem(f"wd_in{j}") for j in range(ESLOTS)]
        consts4, iota4, xturned, xT_ready, g_done, u_done, th_ready, gg_ready, h_ready = map(
            sem, ("consts4", "iota4", "xturned", "exT_ready", "eg_done", "eu_done", "eth_ready", "egg_ready", "eh_ready"))
        y_done, ye_ready, w_ready, added, tok_ready = map(sem, ("ey_done", "ye_ready", "w_ready", "added", "tok_ready"))
        block = ctx.enter_context(nc.Block())

        @block.sync
        def _(sp):
            def load(e, j, first=False):
                if not first:
                    sp.wait_ge(xturned, e - ESLOTS + 1)
                    stand(sp, passed)
                    sp.wait_ge(tok_ready, e - ESLOTS + 2)
                    stand(sp, passed)
                sp.dma_start(rows[j][:, :], xe[bass.ds(e * CAP, CAP), :]).then_inc(rows_in[j], 16)
                if not first:
                    sp.wait_ge(u_done, e - ESLOTS + 1)
                    stand(sp, passed)
                for w, dram in ((wg, wge), (wu, wue)):
                    sp.dma_start(w[j][:, :, :], dram[bass.ds(e, 1), :, :].rearrange("o (k p) f -> p (o k) f", p=P)).then_inc(gu_in[j], 16)
                if not first:
                    sp.wait_ge(y_done, e - ESLOTS + 1)
                    stand(sp, passed)
                sp.dma_start(wd[j][:, 0:2, :], wde[bass.ds(e, 1), 0:2 * P, :].rearrange("o (k p) f -> p (o k) f", p=P)).then_inc(wd_in[j], 16)
                sp.dma_start(wd[j][FPAD:P, 2, :], wde[bass.ds(e, 1), 2 * P:F, :].rearrange("o p f -> (o p) f")).then_inc(wd_in[j], 16)

            for e in range(ESLOTS):
                load(e, e, first=True)
            with sp.Fori(1, E // ESLOTS) as r:
                for j in range(ESLOTS):
                    load(r * ESLOTS + j, j)

        @block.gpsimd
        def _(pool):
            pool.memset(ident[:, :], 0.0).then_inc(iota4, 1)
            for j in range(ESLOTS):
                pool.memset(wd[j][0:FPAD, 2, :], 0.0).then_inc(consts4, 1)
            pool.wait_ge(iota4, 1)
            pool.affine_select(out=ident[:, :], in_=ident[:, :], compare_op=ALU.not_equal, fill=1.0, base=0,
                               pattern=[[-1, P]], channel_multiplier=1).then_inc(consts4, 1)

            def add(r):
                for j in range(2):
                    e = r * 2 + j
                    pool.wait_ge(ye_ready, e + 3)
                    if not isinstance(e, int) or e:
                        pool.wait_ge(added, e * 16)
                    stand(pool, passed)
                    pool.indirect_dma_start(acc, bass.IndirectOffsetOnAxis(tok[j][:, :], 0), ye[j][:, :], None,
                                            bounds_check=T + CAP - 1, oob_is_err=True, compute_op=ALU.add).then_inc(added, 16)

            add(0)
            with pool.Fori(1, E // 2) as r:
                add(r)
            pool.wait_ge(added, E * 16)

        @block.tensor
        def _(pe):
            def turn(r, j):
                pe.wait_ge(rows_in[j], r * 16 + 16)
                stand(pe, passed)
                for k in range(KT):
                    last = pe.transpose(p_x[:, k, 0:CAP], rows[j][:, k * P:(k + 1) * P], ident[0:CAP, 0:CAP])
                last.then_inc(xturned, 1)

            def gate_up(r, j):
                e = r * ESLOTS + j
                pe.wait_ge(gu_in[j], r * 32 + 32)
                pe.wait_ge(xT_ready, e + 1)
                if not isinstance(e, int) or e:
                    pe.wait_ge(h_ready, e)
                for w, p, done in ((wg, p_g, g_done), (wu, p_u, u_done)):
                    for f in range(FN):
                        for k in range(KT):
                            last = pe.matmul(p[:, f, :], w[j][:, k, F0[f]:F0[f] + P], xT[:, k, :], start=(k == 0), stop=(k == KT - 1))
                    last.then_inc(done, 1)

            def down(r, j):
                e = r * ESLOTS + j
                pe.wait_ge(wd_in[j], r * 32 + 32)
                pe.wait_ge(h_ready, e + 1)
                pe.wait_ge(ye_ready, e + 1)
                for f in range(FN):
                    last = pe.matmul(p_y[j % 2][:, :], hT[j % 2][:, f, :], wd[j][:, f, :], start=(f == 0), stop=(f == FN - 1))
                last.then_inc(y_done, 1)

            def round_(r, j, first=False, final=False):
                gate_up(r, j)
                if not final:
                    turn(*((r, j + 1) if j < ESLOTS - 1 else (r + 1, 0)))
                if not first:
                    down(*((r, j - 1) if j else (r - 1, ESLOTS - 1)))

            pe.wait_ge(consts4, ESLOTS + 1)
            turn(0, 0)
            for j in range(ESLOTS):
                round_(0, j, first=j == 0)
            with pe.Fori(1, E // ESLOTS - 1) as r:
                for j in range(ESLOTS):
                    round_(r, j)
            for j in range(ESLOTS):
                round_(E // ESLOTS - 1, j, final=j == ESLOTS - 1)
            down(E // ESLOTS - 1, ESLOTS - 1)

        @block.scalar
        def _(act):
            act.sem_inc(ye_ready, 2)

            def copy_x(e):
                act.wait_ge(xturned, e + 1)
                act.activation(xT[:, :, :], p_x[:, :, 0:CAP], ACT.Copy).then_inc(xT_ready, 1)

            def tanh(e):
                act.wait_ge(g_done, e + 1)
                act.activation(th[:, :, :], p_g[:, :, :], ACT.Tanh, scale=0.5).then_inc(th_ready, 1)

            def weigh(e, j):
                act.wait_ge(y_done, e + 1)
                act.wait_ge(tok_ready, e + 2)
                if not isinstance(e, int) or e >= 2:
                    act.wait_ge(added, e * 16 - 16)
                act.activation(ye[j][:, :], p_y[j][:, :], ACT.Copy, scale=weight[j][:, 0:1]).then_inc(ye_ready, 1)

            copy_x(0)
            for e in range(2):
                tanh(e)
                copy_x(e + 1)
                if e:
                    weigh(e - 1, 0)
            with act.Fori(1, E // 2 - 1) as r:
                for j in range(2):
                    e = r * 2 + j
                    tanh(e)
                    copy_x(e + 1)
                    weigh(e - 1, 1 - j)
            tanh(E - 2)
            copy_x(E - 1)
            weigh(E - 3, 1)
            tanh(E - 1)
            weigh(E - 2, 0)
            weigh(E - 1, 1)

        @block.vector
        def _(dve):
            dve.memset(now[:, :], 0.0).then_inc(tok_ready, 1)

            def some(r):
                for j in range(ESLOTS):
                    e = r * ESLOTS + j
                    dve.wait_ge(th_ready, e + 1)
                    dve.scalar_tensor_tensor(gg[:, :, :], th[:, :, :], 1.0, p_g[:, :, :], ALU.add, ALU.mult).then_inc(gg_ready, 1)
                    dve.wait_ge(gg_ready, e + 1)
                    dve.wait_ge(u_done, e + 1)
                    dve.scalar_tensor_tensor(hT[j % 2][:, :, :], gg[:, :, :], 0.5, p_u[:, :, :], ALU.mult, ALU.mult).then_inc(h_ready, 1)
                    dve.wait_ge(rows_in[j], r * 16 + 16)
                    dve.wait_ge(tok_ready, e + 1)
                    dve.wait_ge(ye_ready, e + 1)
                    if not isinstance(e, int) or e >= 2:
                        dve.wait_ge(added, e * 16 - 16)
                    dve.scalar_tensor_tensor(mine[:, :], rows[j][:, C_E:C_E + TOPK], now[:, 0:1], rows[j][:, C_W:C_W + TOPK],
                                             ALU.is_equal, ALU.mult, accum_out=weight[j % 2][:, 0:1]).then_inc(w_ready, 1)
                    dve.wait_ge(w_ready, e * 2 + 1)
                    dve.tensor_copy(tok[j % 2][:, :], rows[j][:, C_TOK:C_TOK + 1]).then_inc(w_ready, 1)
                    dve.wait_ge(w_ready, e * 2 + 2)
                    dve.tensor_scalar(now[:, :], now[:, :], 1.0, None, ALU.add).then_inc(tok_ready, 1)

            some(0)
            with dve.Fori(1, E // ESLOTS) as r:
                some(r)


def finish(nc, x, od, wo_dram, acc, out):
    with ExitStack() as ctx:
        sb, ps, sem = allocators(nc, ctx, "finish")
        passed = sem("passed")
        wo_raw = sb("wo_raw", [P, KT, D])
        wo = [sb(f"wo_{part}", [P, KT, D], F32R) for part in ("hi", "lo")]
        a = [sb(f"a{j}", [P, TPB, D]) for j in range(2)]
        xs = [sb(f"xs{j}", [P, TPB, D]) for j in range(2)]
        res = [sb(f"res{j}", [P, TPB, D]) for j in range(2)]
        ff = [sb(f"ff{j}", [P, TPB, D]) for j in range(2)]
        aT = [[sb(f"oaT_{part}{j}", [P, KT, P], F32R) for part in ("hi", "lo")] for j in range(2)]
        ident = sb("ident5", [P, P])
        p_t = [ps(f"op_t{j}", [P, KT, P]) for j in range(2)]
        p_y = [ps(f"op_y{j}", [P, D]) for j in range(2)]
        wo_in, consts5, iota5, turned, aT_ready, y_done, xf, done = map(
            sem, ("wo_in", "consts5", "iota5", "oturned", "oaT_ready", "oy_done", "xf", "odone"))
        wo_hi, wo_split, a_hi = map(sem, ("wo_hi", "wo_split", "oa_hi"))
        stored = [sem(f"stored{j}") for j in range(2)]
        a_in = [sem(f"a_in{j}") for j in range(2)]
        xf_in = [sem(f"xf_in{j}") for j in range(2)]
        block = ctx.enter_context(nc.Block())

        @block.sync
        def _(sp):
            sp.dma_start(wo_raw[:, :, :], wo_dram.rearrange("(k p) n -> p k n", p=P)).then_inc(wo_in, 16)
            def load(b, c, j, first=False):
                i = b * BPB + c
                if not first:
                    sp.wait_ge(turned, i * TPB - TPB)
                    stand(sp, passed)
                sp.dma_start(a[j][:, :, :], od[bass.ds(i * BLK, BLK), :].rearrange("(t p) d -> p t d", p=P)).then_inc(a_in[j], 16)
                if not first:
                    sp.wait_ge(done, i * TPB - TPB + 2)
                    stand(sp, passed)
                sp.dma_start(xs[j][:, :, :], x[bass.ds(i * BLK, BLK), :].rearrange("(t p) d -> p t d", p=P)).then_inc(xf_in[j], 16)
                sp.dma_start(ff[j][:, :, :], acc[bass.ds(i * BLK, BLK), :].rearrange("(t p) d -> p t d", p=P)).then_inc(xf_in[j], 16)

            for c in range(2):
                load(0, c, c, first=True)
            for c in range(2, BPB):
                load(0, c, c % 2)
            with sp.Fori(1, B) as b:
                for c in range(BPB):
                    load(b, c, c % 2)

        @block.gpsimd
        def _(pool):
            pool.memset(ident[:, :], 0.0).then_inc(iota5, 1)
            pool.wait_ge(iota5, 1)
            pool.affine_select(out=ident[:, :], in_=ident[:, :], compare_op=ALU.not_equal, fill=1.0, base=0,
                               pattern=[[-1, P]], channel_multiplier=1).then_inc(consts5, 1)

        @block.tensor
        def _(pe):
            def turn(r, j, t):
                if t == 0:
                    pe.wait_ge(a_in[j], r * 16 + 16)
                    stand(pe, passed)
                for k in range(KT):
                    last = pe.transpose(p_t[t % 2][:, k, :], a[j][:, t, k * P:(k + 1) * P], ident[:, :])
                last.then_inc(turned, 1)

            def tile(r, j, t):
                n = (r * 2 + j) * TPB + t
                if t < TPB - 1:
                    turn(r, j, t + 1)
                elif j == 0:
                    turn(r, 1, 0)
                elif not isinstance(r, int):
                    turn(r + 1, 0, 0)
                pe.wait_ge(aT_ready, n + 1)
                pe.wait_ge(done, n + 1)
                for k in range(KT):
                    last = products(pe, p_y[t % 2][:, :], [part[:, k, :] for part in aT[t % 2]], [part[:, k, :] for part in wo],
                                    k == 0, k == KT - 1)
                last.then_inc(y_done, 1)

            pe.wait_ge(consts5, 1)
            turn(0, 0, 0)
            pe.wait_ge(wo_split, KT)
            with pe.Fori(0, NBLK // 2 - 1) as r:
                for j in range(2):
                    for t in range(TPB):
                        tile(r, j, t)
            for j in range(2):
                for t in range(TPB):
                    tile(NBLK // 2 - 1, j, t)

        @block.scalar
        def _(act):
            act.wait_ge(wo_in, 16)
            for k in range(KT):
                act.activation(wo[0][:, k, :], wo_raw[:, k, :], ACT.Copy).then_inc(wo_hi, 1)

            def store(r, j):
                act.wait_ge(done, (r * 2 + j) * TPB + TPB + 2)
                act.dma_start(out[bass.ds((r * 2 + j) * BLK, BLK), :].rearrange("(t p) d -> p t d", p=P), res[j][:, :, :]).then_inc(stored[j], 16)

            def blocks(r, first=False):
                for j in range(2):
                    for t in range(TPB):
                        act.wait_ge(turned, (r * 2 + j) * TPB + t + 1)
                        act.activation(aT[t % 2][0][:, :, :], p_t[t % 2][:, :, :], ACT.Copy).then_inc(a_hi, 1)
                        if t == 1 and j:
                            store(r, 0)
                        elif t == 1 and not first:
                            store(r - 1, 1)

            blocks(0, first=True)
            with act.Fori(1, NBLK // 2) as r:
                blocks(r)
            store(NBLK // 2 - 1, 1)
            for j in range(2):
                act.wait_ge(stored[j], NBLK // 2 * 16)

        @block.vector
        def _(dve):
            def rest(n, t):
                dve.wait_ge(a_hi, n + 1)
                dve.tensor_tensor(aT[t % 2][1][:, :, :], p_t[t % 2][:, :, :], aT[t % 2][0][:, :, :].bitcast(F32), ALU.subtract)\
                   .then_inc(aT_ready, 1)

            def tile(r, j, t, last=True):
                n = (r * 2 + j) * TPB + t
                if not (isinstance(r, int) and last and j == 1 and t == TPB - 1):
                    rest(n + 1, t + 1)
                if t == 0:
                    dve.wait_ge(xf_in[j], r * 32 + 32)
                    if not isinstance(r, int) or r:
                        dve.wait_ge(stored[j], r * 16)
                dve.tensor_tensor(xs[j][:, t, :], xs[j][:, t, :], ff[j][:, t, :], ALU.add).then_inc(xf, 1)
                dve.wait_ge(xf, n + 1)
                dve.wait_ge(y_done, n + 1)
                dve.tensor_tensor(res[j][:, t, :], p_y[t % 2][:, :], xs[j][:, t, :], ALU.add).then_inc(done, 1)

            dve.sem_inc(done, 2)
            for k in range(KT):
                dve.wait_ge(wo_hi, k + 1)
                dve.tensor_tensor(wo[1][:, k, :], wo_raw[:, k, :], wo[0][:, k, :].bitcast(F32), ALU.subtract).then_inc(wo_split, 1)
            rest(0, 0)
            for j in range(2):
                for t in range(TPB):
                    tile(0, j, t, last=False)
            with dve.Fori(1, NBLK // 2 - 1) as r:
                for j in range(2):
                    for t in range(TPB):
                        tile(r, j, t)
            for j in range(2):
                for t in range(TPB):
                    tile(NBLK // 2 - 1, j, t)


def build(nc, x, wq1, wk1, wq2, wk2, wv, wo, lam, wr, wge, wue, wde, wsg, wsu, wsd, out):
    def dram(name, shape):
        return nc.dram_tensor(name, shape, F32, kind="Internal").ap()

    xe = dram("xe", [E * CAP, ROW])
    xnt_d = dram("xnt_d", [NSB, P, 2, KT, SBLK])
    qd = dram("qd", [B, H, BPB, 2 * DH, 2, BLK])
    kd = dram("kd", [B, H, 2 * DH, 2, S])
    vd = dram("vd", [B, H, P, S // P, DH])
    gate_d = dram("gate_d", [P, NBLK * TPB])
    od = dram("od", [T, D])
    acc = dram("acc", [T + CAP, D])
    project(nc, x, (wq1, wk1, wq2, wk2, wv), wr, xe, xnt_d, qd, kd, vd, gate_d)
    attend(nc, qd.rearrange("b h c p m t -> (b h c) p m t"), kd.rearrange("b h p m t -> (b h) p m t"),
           vd.rearrange("b h p t d -> (b h) p t d"), lam, od.rearrange("(b c t p) (h d) -> b c t p h d", b=B, c=BPB, t=TPB, h=H))
    shared(nc, xnt_d, gate_d, wsg, wsu, wsd, acc)
    experts(nc, xe, wge, wue, wde, acc)
    finish(nc, x, od, wo, acc, out)


def kernel(**inputs):
    import numpy as np
    import concourse.bacc as bacc
    from concourse.bass_utils import run_bass_kernel_spmd

    a = {n: np.asarray(v) for n, v in inputs.items()}
    turned = [np.ascontiguousarray(a[f"L0_attn_{n}_w"].T) for n in ("q1", "k1", "q2", "k2", "v", "o")]
    arrays = {
        "x": np.ascontiguousarray(a["L0_attn_x"].reshape(T, D)),
        "wq1": turned[0], "wk1": turned[1], "wq2": turned[2], "wk2": turned[3], "wv": turned[4], "wo": turned[5],
        "lam": np.ascontiguousarray(a["L0_attn_lambda_param"].reshape(1, H)),
        "wr": np.ascontiguousarray(np.concatenate([a["L0_ffn_Wr"], a["L0_ffn_Wse"]], axis=1)),
        "wge": a["L0_ffn_Wg"], "wue": a["L0_ffn_Wu"], "wde": a["L0_ffn_Wd"],
        "wsg": a["L0_ffn_Wsg"], "wsu": a["L0_ffn_Wsu"], "wsd": a["L0_ffn_Wsd"],
    }
    nc = bacc.Bacc("TRN2", target_bir_lowering=False, num_devices=1)
    args = [nc.dram_tensor(f"in_{n}", v.shape, F32, kind="ExternalInput").ap() for n, v in arrays.items()]
    out = nc.dram_tensor("out", [T, D], F32, kind="ExternalOutput").ap()
    build(nc, *args, out)
    r = run_bass_kernel_spmd(nc, [{f"in_{n}": v for n, v in arrays.items()}], core_ids=[0])
    return np.asarray(r.results[0]["out"]).reshape(B, S, D)
```
